# Optimizing a Trainium2 kernel written in Bass

```python
import numpy as np
import jax
import jax.numpy as jnp

def _softmax(x, axis=-1):
    return jax.nn.softmax(x, axis=axis)

def _gelu(x):
    return jax.nn.gelu(x, approximate=True)

def _silu(x):
    return jax.nn.silu(x)

def _sigmoid(x):
    return jax.nn.sigmoid(x)

def _layernorm(x, axis=-1, eps=1e-05):
    m = jnp.mean(x, axis=axis, keepdims=True)
    v = jnp.var(x, axis=axis, keepdims=True)
    return (x - m) / jnp.sqrt(v + eps)

def _scatter_add(tgt, idx, src, axis=0):
    return tgt.at[idx].add(src)

def _segment_sum(src, seg, n):
    return jax.ops.segment_sum(src, seg, n)
kernel_name = 'mk_adj_ffn_d1_adj_r2_86e5a4'

def setup_inputs(seed: int=0):
    np.random.seed(seed)
    _w = jnp.asarray

    def _rec_inputs():
        import jax
        import jax.numpy as jnp
        _gk = jax.random.key(seed)
        x = -0.001547 + 1.001 * jax.random.normal(jax.random.fold_in(_gk, 1), (512, 128), jnp.float32)
        _a = jax.random.bernoulli(jax.random.fold_in(_gk, 2), 0.015625, (512, 512))
        _a = jnp.logical_or(_a, jnp.swapaxes(_a, -1, -2))
        _a = jnp.logical_or(_a, jnp.eye(512, dtype=bool))
        adj = _a.astype(jnp.int32)
        return (x, adj)
    x, adj = _rec_inputs()

    def _L0_gnn_setup():
        import jax, jax.numpy as jnp
        import numpy as np
        BT, BN, D, H = (512, 512, 128, 8)
        DH = D // H
        key = jax.random.key(seed)
        ks = jax.random.split(key, 16)
        s = 1.0 / np.sqrt(D)
        return {'h_target': jax.random.normal(ks[0], (BT, D), jnp.float32), 'h_neigh': jax.random.normal(ks[1], (BN, D), jnp.float32), 'adjacency': jax.random.randint(ks[2], (BT, BN), 0, 2, jnp.int32), 'edge_types': jax.random.randint(ks[3], (BT, BN), 0, 2, jnp.int32), 'Wq': jax.random.normal(ks[4], (D, D), jnp.float32) * s, 'bq': jnp.zeros((D,), jnp.float32), 'Wk': jax.random.normal(ks[5], (D, D), jnp.float32) * s, 'bk': jnp.zeros((D,), jnp.float32), 'Wv': jax.random.normal(ks[6], (D, D), jnp.float32) * s, 'bv': jnp.zeros((D,), jnp.float32), 'Wo': jax.random.normal(ks[7], (D, D), jnp.float32) * s, 'bo': jnp.zeros((D,), jnp.float32), 'E': jax.random.normal(ks[8], (2, D), jnp.float32)}
    _L0_gnn_all = _L0_gnn_setup()
    _L0_gnn_in = {k: v for k, v in _L0_gnn_all.items() if k in ('h_neigh', 'Wq', 'bq', 'Wk', 'bk', 'Wv', 'bv', 'Wo', 'bo', 'E')}
    del _L0_gnn_all

    def _L0_ffn_setup():
        import jax, jax.numpy as jnp
        import numpy as np
        TOP_K = 2
        LN_EPS = 1e-05
        key = jax.random.key(seed)
        ks = jax.random.split(key, 8)
        B, S, D, E, H = (16, 512, 128, 8, 512)
        x = jax.random.normal(ks[0], (B, S, D), dtype=jnp.float32)
        Wr = jax.random.normal(ks[1], (D, E), dtype=jnp.float32) * 0.1
        br = jnp.zeros((E,), dtype=jnp.float32)
        ln_g = jnp.ones((E, D), dtype=jnp.float32)
        ln_b = jnp.zeros((E, D), dtype=jnp.float32)
        W1 = jax.random.normal(ks[2], (E, D, H), dtype=jnp.float32) * (1.0 / np.sqrt(D))
        b1 = jnp.zeros((E, H), dtype=jnp.float32)
        W2 = jax.random.normal(ks[3], (E, H, D), dtype=jnp.float32) * (1.0 / np.sqrt(H))
        b2 = jnp.zeros((E, D), dtype=jnp.float32)
        return {'x': x, 'Wr': Wr, 'br': br, 'ln_g': ln_g, 'ln_b': ln_b, 'W1': W1, 'b1': b1, 'W2': W2, 'b2': b2}
    _L0_ffn_all = _L0_ffn_setup()
    _L0_ffn_in = {k: v for k, v in _L0_ffn_all.items() if k in ('Wr', 'br', 'ln_g', 'ln_b', 'W1', 'b1', 'W2', 'b2')}
    del _L0_ffn_all
    return {'x': x, 'adj': adj, 'L0_gnn_h_neigh': _L0_gnn_in['h_neigh'], 'L0_gnn_Wq': _L0_gnn_in['Wq'], 'L0_gnn_bq': _L0_gnn_in['bq'], 'L0_gnn_Wk': _L0_gnn_in['Wk'], 'L0_gnn_bk': _L0_gnn_in['bk'], 'L0_gnn_Wv': _L0_gnn_in['Wv'], 'L0_gnn_bv': _L0_gnn_in['bv'], 'L0_gnn_Wo': _L0_gnn_in['Wo'], 'L0_gnn_bo': _L0_gnn_in['bo'], 'L0_gnn_E': _L0_gnn_in['E'], 'L0_ffn_Wr': _L0_ffn_in['Wr'], 'L0_ffn_br': _L0_ffn_in['br'], 'L0_ffn_ln_g': _L0_ffn_in['ln_g'], 'L0_ffn_ln_b': _L0_ffn_in['ln_b'], 'L0_ffn_W1': _L0_ffn_in['W1'], 'L0_ffn_b1': _L0_ffn_in['b1'], 'L0_ffn_W2': _L0_ffn_in['W2'], 'L0_ffn_b2': _L0_ffn_in['b2']}

def reference(x, adj, L0_gnn_h_neigh, L0_gnn_Wq, L0_gnn_bq, L0_gnn_Wk, L0_gnn_bk, L0_gnn_Wv, L0_gnn_bv, L0_gnn_Wo, L0_gnn_bo, L0_gnn_E, L0_ffn_Wr, L0_ffn_br, L0_ffn_ln_g, L0_ffn_ln_b, L0_ffn_W1, L0_ffn_b1, L0_ffn_W2, L0_ffn_b2):
    import jax
    import jax.numpy as jnp

    def _L0_gnn_ref(h_target, h_neigh, adjacency, edge_types, Wq, bq, Wk, bk, Wv, bv, Wo, bo, E):
        import jax, jax.numpy as jnp
        import numpy as np
        BT, BN, D, H = (512, 512, 128, 8)
        DH = D // H
        Bt, d = h_target.shape
        Bn = h_neigh.shape[0]
        msg = h_neigh[None, :, :] + E[edge_types]
        q = (h_target @ Wq.T + bq).reshape(Bt, H, DH)
        k = (msg @ Wk.T + bk).reshape(Bt, Bn, H, DH)
        v = (msg @ Wv.T + bv).reshape(Bt, Bn, H, DH)
        scores = jnp.einsum('bhd,bnhd->bhn', q, k) / np.sqrt(DH).astype(np.float32)
        mask = adjacency[:, None, :] == 0
        scores = jnp.where(mask, jnp.float32(-1000000000.0), scores)
        attn = jax.nn.softmax(scores, axis=-1)
        attn = jnp.where(mask, jnp.float32(0.0), attn)
        out = jnp.einsum('bhn,bnhd->bhd', attn, v).reshape(Bt, d)
        return out @ Wo.T + bo

    def _L0_ffn_ref(x, Wr, br, ln_g, ln_b, W1, b1, W2, b2):
        import jax, jax.numpy as jnp
        import numpy as np
        TOP_K = 2
        LN_EPS = 1e-05
        B, S, D = x.shape
        N = B * S
        xt = x.reshape(N, D)
        logits = xt @ Wr + br
        probs = jax.nn.softmax(logits, axis=-1)
        top_p, top_idx = jax.lax.top_k(probs, TOP_K)
        weights = top_p / top_p.sum(axis=-1, keepdims=True)
        mu = xt.mean(axis=-1, keepdims=True)
        var = ((xt - mu) ** 2).mean(axis=-1, keepdims=True)
        xn = (xt - mu) * jax.lax.rsqrt(var + LN_EPS)
        xe = xn[None, :, :] * ln_g[:, None, :] + ln_b[:, None, :]
        h = jax.nn.gelu(jnp.einsum('end,edh->enh', xe, W1) + b1[:, None, :], approximate=False)
        y = jnp.einsum('enh,ehd->end', h, W2) + b2[:, None, :]
        y_tok = jnp.transpose(y, (1, 0, 2))
        sel = jnp.take_along_axis(y_tok, top_idx[:, :, None], axis=1)
        out = (weights[:, :, None] * sel).sum(axis=1)
        return out.reshape(B, S, D)
    x = x + _L0_gnn_ref(_layernorm(x, axis=-1), L0_gnn_h_neigh, adj, adj, L0_gnn_Wq, L0_gnn_bq, L0_gnn_Wk, L0_gnn_bk, L0_gnn_Wv, L0_gnn_bv, L0_gnn_Wo, L0_gnn_bo, L0_gnn_E)
    x = x + _L0_ffn_ref(_layernorm(x, axis=-1)[None], L0_ffn_Wr, L0_ffn_br, L0_ffn_ln_g, L0_ffn_ln_b, L0_ffn_W1, L0_ffn_b1, L0_ffn_W2, L0_ffn_b2)[0]
    return x

_drawn_inputs = setup_inputs


def setup_inputs(seed=0):
    import zlib

    import numpy as np

    out = dict(_drawn_inputs(seed))
    spreads = {'L0_gnn_bq': (0.0, 0.1),
     'L0_gnn_bk': (0.0, 0.1),
     'L0_gnn_bv': (0.0, 0.1),
     'L0_gnn_bo': (0.0, 0.1),
     'L0_ffn_br': (0.0, 0.1),
     'L0_ffn_ln_g': (1.0, 0.2),
     'L0_ffn_ln_b': (0.0, 0.1),
     'L0_ffn_b1': (0.0, 0.1),
     'L0_ffn_b2': (0.0, 0.1)}
    factors = {}
    for name, (base, spread) in spreads.items():
        noise = np.random.default_rng([zlib.crc32(name.encode()), seed]).standard_normal(out[name].shape)
        drawn = base * np.exp(spread * noise) if base else spread * noise
        out[name] = jnp.asarray(drawn.astype(out[name].dtype))
    for name, factor in factors.items():
        out[name] = (out[name] * factor).astype(out[name].dtype)
    return out
```

```python
from contextlib import ExitStack

import concourse.bass as bass
from concourse import mybir

ALU = mybir.AluOpType
ACT = mybir.ActivationFunctionType
F32 = mybir.dt.float32
F32R = mybir.dt.float32r
BF16 = mybir.dt.bfloat16
I32 = mybir.dt.int32
U32 = mybir.dt.uint32

P = 128
EPS = 1e-5
MASKED = -1e9
LOWEST_MAX = -1e8
TINY = 1e-30
HEAD_ROWS = 32
PARTS = 2


def gnn_ffn_kernel(nc, x, adj, h_neigh, Wq, bq, Wk, bk, Wv, bv, Wo, bo, E, Wr, br, ln_g, ln_b, W1, b1, W2, b2, out):
    T, D = x.shape
    N = h_neigh.shape[0]
    NE, _, F = W1.shape
    NT, NI, FC = T // P, N // P, F // P
    DH = 16
    H = D // DH
    G = 4
    NG = H // G
    HT = 2
    NHALF = NT // HT
    TOK = HT * P
    NU = NHALF * NG
    KROWS = 96
    MAXROW = 4 * DH
    assert D == P and N == 512 and T == 512 and H == 8

    NS_U = HT * G
    NIP = NI // 2
    NX_U = NIP * G
    LEAD = NS_U + 4
    NP_RING = 2 * G
    NH_RING = 8
    HALF_E = NE * FC

    R_B1, R_G, R_B, R_BQ, R_BK, R_E1 = 0, NE * FC, NE * FC + NE, NE * FC + 2 * NE, NE * FC + 2 * NE + 1, NE * FC + 2 * NE + 2
    NROWS = R_E1 + 1

    with ExitStack() as ctx:
        def sb(name, shape, dt):
            return ctx.enter_context(nc.sbuf_tensor(name, shape, dt))

        def sem(name):
            return ctx.enter_context(nc.semaphore(name))

        bank = [ctx.enter_context(nc.psum_tensor(f"bank{i}", [P, 512], F32)) for i in range(8)]
        S_BANK, X_BANK, O_BANK, MISC = [0, 1], [2, 3, 4], [5, 6], 7

        x_sb = sb("x_sb", [P, NT, D], F32)
        adj_sb = sb("adj_sb", [P, NT, N], I32)
        hn_sb = sb("hn_sb", [P, NI, D], F32)
        w_sb = sb("w_sb", [P, 3, D], F32)
        wo_sb = sb("wo_sb", [P, D], F32)
        rows = sb("rows", [NROWS, D], F32)
        bv_bc = sb("bv_bc", [P, D], F32)
        bo_bc = sb("bo_bc", [P, D], F32)
        br_bc = sb("br_bc", [P, NE], F32)
        wr_sb = sb("wr_sb", [P, NE], F32)
        b2_sb = sb("b2_sb", [NE, D], F32)
        w1_sb = sb("w1_sb", [P, NE, F], F32)
        w2_sb = sb("w2_sb", [P, NE, FC, D], F32)
        ident = sb("ident", [P, P], F32)
        identb = sb("identb", [P, P], BF16)
        ones_pick = sb("ones_pick", [P, P], F32)
        pick_q = sb("pick_q", [P, PARTS, H, MAXROW], F32R)
        pick_k = sb("pick_k", [P, PARTS, H, MAXROW], F32R)
        half_pow = sb("half_pow", [P, HT * 4], F32)
        euler = sb("euler", [P, HT], F32)
        expert_no = sb("expert_no", [P, NE], F32)
        stats = sb("stats", [P, NT, 6], F32)
        mv = sb("mv", [P, NT, 2], F32)
        var_eps = sb("var_eps", [P, NT], F32)
        rstd = sb("rstd", [P, NT], F32)
        xn1 = sb("xn1", [P, NT, D], F32)
        xb = sb("xb", [P, NT, D], F32)
        xn1T = sb("xn1T", [P, T], F32)
        wT = sb("wT", [P, 4, D], F32)
        cols = sb("cols", [P, NROWS], F32)
        msgT = sb("msgT", [P, N], F32)
        q_full = sb("q_full", [P, T], F32)
        k_full = sb("k_full", [P, N], F32)
        q_part = sb("q_part", [P, PARTS, T], F32R)
        k_part = sb("k_part", [P, PARTS, N], F32R)
        QA = sb("QA", [KROWS, H, T], F32R)
        KA = sb("KA", [KROWS, H, N], F32R)
        Va = sb("Va", [P, NI, H, HEAD_ROWS], F32)
        maskb = sb("maskb", [P, NT, N], BF16)
        maskT = sb("maskT", [P, NI, T], BF16)
        junk = sb("junk", [P, 2, N], BF16)
        mx = sb("mx", [P, NU, NS_U], F32)
        nmax = sb("nmax", [P, NU, NS_U], F32)
        nmax_part = sb("nmax_part", [P, NU, HT, PARTS, G], F32R)
        nmaxT = sb("nmaxT", [PARTS * G, NU, TOK], F32)
        PT = sb("PT", [P, NP_RING, 512], F32)
        O_sb = sb("O_sb", [P, NU, TOK], F32)
        den = sb("den", [P, NU, HT * G], F32)
        rden = sb("rden", [P, NU, HT * G], F32)
        o_nat = sb("o_nat", [P, NHALF, HT, H, DH], F32)
        o_natT = sb("o_natT", [P, NHALF, TOK], F32)
        x2 = sb("x2", [P, NT, D], F32)
        stats2 = sb("stats2", [P, NT, 6], F32)
        mv2 = sb("mv2", [P, NT, 2], F32)
        va = sb("va", [P, NT], F32)
        ra = sb("ra", [P, NT], F32)
        ra2 = sb("ra2", [P, NT], F32)
        vb = sb("vb", [P, NT], F32)
        rb = sb("rb", [P, NT], F32)
        rab = sb("rab", [P, NT], F32)
        sdb = sb("sdb", [P, NT], F32)
        xn2 = sb("xn2", [P, NT, D], F32)
        xn2T = sb("xn2T", [P, NHALF, TOK], F32)
        logits = sb("logits", [P, NT, NE], F32)
        top = sb("top", [P, NT, 8], F32)
        top_at = sb("top_at", [P, NT, 8], U32)
        top_no = sb("top_no", [P, NT, 2], F32)
        gap = sb("gap", [P, NT], F32)
        egap = sb("egap", [P, NT], F32)
        dgap = sb("dgap", [P, NT], F32)
        wtop = sb("wtop", [P, NT, 2], F32)
        wfirst = sb("wfirst", [P, NT, NE], F32)
        wsecond = sb("wsecond", [P, NT, NE], F32)
        wexp = sb("wexp", [P, NT, NE], F32)
        wexpT = sb("wexpT", [NE, NHALF, TOK], F32)
        w1_part = sb("w1_part", [P, NE, PARTS, F], F32R)
        xe = sb("xe", [P, 2, TOK], F32)
        xe_part = sb("xe_part", [P, 2, PARTS, TOK], F32R)
        hid = PT[:, :, 0:TOK]
        acc = sb("acc", [P, 2, NT, D], F32)

        in_x, in_hn, in_w, in_wo, in_rows, in_bc, in_adj = (sem(n) for n in ("in_x", "in_hn", "in_w", "in_wo", "in_rows", "in_bc", "in_adj"))
        in_small, in_w1, in_w2 = sem("in_small"), [sem(f"in_w1_{e}") for e in range(NE)], [sem(f"in_w2_{e}") for e in range(NE)]
        ident_ready, pick_zero, pick_ready, const_ready, pool_step = sem("ident_ready"), sem("pick_zero"), sem("pick_ready"), sem("const_ready"), sem("pool_step")
        dve_step, act_step = sem("dve_step"), sem("act_step")
        var1_ready, rstd1_ready, xn1_ready, xn1T_ready = sem("var1_ready"), sem("rstd1_ready"), sem("xn1_ready"), sem("xn1T_ready")
        xT_done, w_done, hT_done, rows_done, wo_done, q_done, k_done, v_done, mT_done = (
            sem(n) for n in ("xT_done", "w_done", "hT_done", "rows_done", "wo_done", "q_done", "k_done", "v_done", "mT_done"))
        wT_ready, cols_ready, msgT_ready, kfull_ready, qpart_ready, kpart_ready = (
            sem(n) for n in ("wT_ready", "cols_ready", "msgT_ready", "kfull_ready", "qpart_ready", "kpart_ready"))
        va_ready, maskb_ready, maskT_ready, woT_ready, xb_ready = (
            sem(n) for n in ("va_ready", "maskb_ready", "maskT_ready", "woT_ready", "xb_ready"))
        picked, heads_ready = sem("picked"), sem("heads_ready")
        s_done, s_used = sem("s_done"), sem("s_used")
        nmax_ready, nmaxT_done, nmaxT_ready, nmax_in = sem("nmax_ready"), sem("nmaxT_done"), sem("nmaxT_ready"), sem("nmax_in")
        st_done, exp_done, pv_done, o_ready = sem("st_done"), sem("exp_done"), sem("pv_done"), sem("o_ready")
        oT_done, onat_ready, onatT_done, onatT_ready, proj_done, x2_ready = (
            sem(n) for n in ("oT_done", "onat_ready", "onatT_done", "onatT_ready", "proj_done", "x2_ready"))
        va2_ready, ra_ready, vb_ready, rb_ready, xn2_ready, xn2T_done, xn2T_ready = (
            sem(n) for n in ("va2_ready", "ra_ready", "vb_ready", "rb_ready", "xn2_ready", "xn2T_done", "xn2T_ready"))
        logits_done, gap_ready, egap_ready, wexp_ready, wexpT_done, wexpT_ready, b2_done, acc0_ready, logits_used = (
            sem(n) for n in ("logits_done", "gap_ready", "egap_ready", "wexp_ready", "wexpT_done", "wexpT_ready", "b2_done", "acc0_ready", "logits_used"))
        oT_used = sem("oT_used")
        w1hi_ready, w1part_ready, xe_ready, f1_done, hid_ready, f2_done, y_used, stored = (
            sem(n) for n in ("w1hi_ready", "w1part_ready", "xe_ready", "f1_done", "hid_ready", "f2_done", "y_used", "stored"))

        block = ctx.enter_context(nc.Block())

        unit = [(half, g) for half in range(NHALF) for g in range(NG)]

        @block.sync
        def _(sp):
            sp.dma_start(x_sb[:], x.rearrange("(t p) d -> p t d", p=P)).then_inc(in_x, 16)
            sp.dma_start(w_sb[:, 0, :], Wq).then_inc(in_w, 16)
            sp.dma_start(bo_bc[:], bo.partition_broadcast(P)).then_inc(in_bc, 16)
            sp.dma_start(bv_bc[:], bv.partition_broadcast(P)).then_inc(in_bc, 16)
            sp.dma_start(br_bc[:], br.partition_broadcast(P)).then_inc(in_bc, 16)
            for t in range(NT):
                sp.dma_start(adj_sb[:, t, :], adj[t * P:(t + 1) * P, :]).then_inc(in_adj, 16)
            sp.dma_start(wr_sb[:], Wr).then_inc(in_small, 16)
            sp.dma_start(b2_sb[:], b2).then_inc(in_small, 16)
            for e in range(NE):
                sp.dma_start(w1_sb[:, e, :], W1[e]).then_inc(in_w1[e], 16)
            for u, (half, g) in enumerate(unit):
                sp.wait_ge(nmaxT_ready, u + 1)
                for part in range(PARTS):
                    sp.dma_start(QA[MAXROW + part:MAXROW + part + 1, G * g:G * g + G, half * TOK:(half + 1) * TOK].bitcast(F32),
                                 nmaxT[G * part:G * part + G, u, :]).then_inc(nmax_in, 16)
                if u < NE // 2:
                    for e in (2 * u, 2 * u + 1):
                        sp.dma_start(w2_sb[:, e, :, :], W2[e].rearrange("(c p) d -> p c d", p=P)).then_inc(in_w2[e], 16)
            for half in range(NHALF):
                sp.wait_ge(y_used, NE * (half + 1))
                sp.dma_start(out[half * TOK:(half + 1) * TOK, :].rearrange("(t p) d -> p t d", p=P),
                             acc[:, (NE - 1) % 2, half * HT:(half + 1) * HT, :]).then_inc(stored, 16)
            sp.wait_ge(stored, 16 * NHALF)

        @block.gpsimd
        def _(pool):
            steps = [0]

            def step(ins):
                steps[0] += 1
                ins.then_inc(pool_step, 1)
                pool.wait_ge(pool_step, steps[0])

            pool.memset(half_pow[:, 0:NT], -0.5)
            pool.memset(half_pow[:, NT:2 * NT], 0.5)
            pool.memset(euler[:], 2.718281828459045)
            step(pool.memset(ident[:], 0.0))
            pool.affine_select(out=ident[:], in_=ident[:], compare_op=ALU.not_equal, fill=1.0, base=0,
                               pattern=[[-1, P]], channel_multiplier=1).then_inc(ident_ready, 1)
            step(pool.memset(identb[:], 0.0))
            pool.affine_select(out=identb[:], in_=identb[:], compare_op=ALU.not_equal, fill=1.0, base=0,
                               pattern=[[-1, P]], channel_multiplier=1).then_inc(ident_ready, 1)
            pool.memset(pick_q[:].bitcast(F32), 0.0).then_inc(pick_zero, 1)
            pool.memset(pick_k[:].bitcast(F32), 0.0).then_inc(pick_zero, 1)
            pool.wait_ge(var1_ready, 1)
            pool.tensor_tensor(rstd[:], var_eps[:], half_pow[:, 0:NT], ALU.pow).then_inc(rstd1_ready, 1)
            pool.memset(Va[:], 0.0).then_inc(const_ready, 1)
            pool.wait_ge(const_ready, 1)
            pool.memset(Va[:, :, :, DH:DH + 1], 1.0).then_inc(const_ready, 1)
            pool.wait_ge(const_ready, 2)
            pool.memset(QA[MAXROW:KROWS, :, :].bitcast(F32), 0.0).then_inc(const_ready, 1)
            pool.wait_ge(const_ready, 3)
            step(pool.memset(KA[MAXROW:KROWS, :, :].bitcast(F32), 0.0))
            pool.memset(KA[MAXROW:MAXROW + PARTS, :, :].bitcast(F32), 1.0).then_inc(const_ready, 1)
            pool.wait_ge(const_ready, 4)
            pool.iota(expert_no[:], pattern=[[1, NE]], base=0, channel_multiplier=0,
                      allow_small_or_imprecise_dtypes=True).then_inc(const_ready, 1)
            pool.wait_ge(in_x, 16)
            pool.wait_ge(in_bc, 48)
            for t in range(NT):
                last = pool.tensor_tensor(xb[:, t, :], x_sb[:, t, :], bo_bc[:], ALU.add)
            last.then_inc(xb_ready, 1)
            def w1_rest(e):
                pool.wait_ge(w1hi_ready, e + 1)
                pool.tensor_tensor(w1_part[:, e, 1, :], w1_sb[:, e, :], w1_part[:, e, 0, :].bitcast(F32),
                                   ALU.subtract).then_inc(w1part_ready, 1)

            for e in range(NE // 2):
                w1_rest(e)
            for half in range(NHALF):
                ts = slice(half * HT, (half + 1) * HT)
                pool.wait_ge(va2_ready, half + 1)
                pool.tensor_tensor(ra[:, ts], va[:, ts], half_pow[:, 0:HT], ALU.pow).then_inc(ra_ready, 1)
                pool.wait_ge(vb_ready, half + 1)
                pool.tensor_tensor(rb[:, ts], vb[:, ts], half_pow[:, 0:HT], ALU.pow).then_inc(rb_ready, 1)
                pool.wait_ge(gap_ready, half + 1)
                pool.tensor_tensor(egap[:, ts], euler[:], gap[:, ts], ALU.pow).then_inc(egap_ready, 1)
                if half == 0:
                    for e in range(NE // 2, NE):
                        w1_rest(e)

        @block.tensor
        def _(pe):
            misc_uses = [(cols_ready, 1)]

            pe.wait_ge(ident_ready, 1)
            pe.wait_ge(in_hn, 16)
            for i in range(NI):
                last = pe.transpose(bank[2][:, i * P:(i + 1) * P], hn_sb[:, i, :], ident[:])
            last.then_inc(hT_done, 1)
            pe.wait_ge(in_rows, 16 * 6)
            pe.transpose(bank[MISC][:, 0:NROWS], rows[:], ident[0:NROWS, 0:NROWS]).then_inc(rows_done, 1)
            pe.wait_ge(in_w, 48)
            for k in range(3):
                pe.transpose(bank[1][:, k * P:(k + 1) * P], w_sb[:, k, :], ident[:])
            pe.wait_ge(in_wo, 16)
            pe.transpose(bank[1][:, 3 * P:4 * P], wo_sb[:], ident[:]).then_inc(w_done, 1)
            pe.wait_ge(xn1_ready, 1)
            for t in range(NT):
                last = pe.transpose(bank[0][:, t * P:(t + 1) * P], xn1[:, t, :], ident[:])
            last.then_inc(xT_done, 1)
            pe.wait_ge(wT_ready, 1)
            pe.wait_ge(msgT_ready, 1)
            pe.matmul(bank[4][:], wT[:, 1, :], msgT[:], start=True, stop=True).then_inc(k_done, 1)
            pe.wait_ge(xn1T_ready, 1)
            pe.matmul(bank[3][:], wT[:, 0, :], xn1T[:], start=True, stop=True).then_inc(q_done, 1)
            for i in range(NI):
                last = pe.matmul(bank[5][:, i * P:(i + 1) * P], msgT[:, i * P:(i + 1) * P], wT[:, 2, :], start=True, stop=True)
            last.then_inc(v_done, 1)

            def pick(n):
                pair, what = n // 2, n % 2
                src, pick_w, part_ready = ((k_part, pick_k, kpart_ready), (q_part, pick_q, qpart_ready))[what]
                pe.wait_ge(part_ready, 1)
                pe.wait_ge(pick_ready, 2 * PARTS)
                if n >= 2:
                    pe.wait_ge(heads_ready, 2 * (n - 1))
                b = bank[4 - n % 2]
                for part in range(PARTS):
                    last = pe.matmul(b[:], pick_w[:, part, 2 * pair:2 * pair + 2, :].rearrange("p a r -> p (a r)"), src[:, part, :], start=(part == 0), stop=(part == PARTS - 1))
                last.then_inc(picked, 1)

            def score(n):
                u, r = n // NS_U, n % NS_U
                half, g = unit[u]
                t, j = half * HT + r // G, r % G
                if r // G == 0 and half == 0:
                    pe.wait_ge(heads_ready, 4 * ((G * g + j) // 2) + 2 + 1 + (j % 2))
                if n >= 2:
                    pe.wait_ge(s_used, n - 1)
                pe.matmul(bank[S_BANK[n % 2]][:], QA[:, G * g + j, t * P:(t + 1) * P], KA[:, G * g + j, :],
                          start=True, stop=True).then_inc(s_done, 1)

            def transpose_maxima(u):
                pe.wait_ge(nmax_ready, u + 1)
                misc_free()
                for t in range(HT):
                    last = pe.transpose(bank[MISC][0:PARTS * G, t * P:(t + 1) * P],
                                        nmax_part[:, u, t, :, :].bitcast(F32).rearrange("p a b -> p (a b)"), ident[:])
                last.then_inc(nmaxT_done, 1)
                misc_uses.append((nmaxT_ready, u + 1))

            def misc_free():
                if misc_uses:
                    pe.wait_ge(*misc_uses[-1])

            def transposed_scores(n):
                u, r = n // NX_U, n % NX_U
                half, g = unit[u]
                ip, head = r // G, G * g + r % G
                if r == 0:
                    pe.wait_ge(nmax_in, 16 * PARTS * (u + 1))
                if n == 0:
                    pe.wait_ge(maskT_ready, 2)
                    pe.wait_ge(heads_ready, 2 * H)
                if n >= len(X_BANK):
                    pe.wait_ge(exp_done, n - len(X_BANK) + 1)
                b = bank[X_BANK[n % len(X_BANK)]]
                pe.matmul(b[:], identb[:], maskT[:, 2 * ip:2 * ip + 2, half * TOK:(half + 1) * TOK], start=True, stop=False)
                for k in range(2):
                    i = 2 * ip + k
                    last = pe.matmul(b[:, k * TOK:(k + 1) * TOK], KA[:, head, i * P:(i + 1) * P],
                                     QA[:, head, half * TOK:(half + 1) * TOK], start=False, stop=(k == 1))
                last.then_inc(st_done, 1)

            def weighted_values(q):
                u, ip = q // NIP, q % NIP
                half, g = unit[u]
                if q == 0:
                    pe.wait_ge(va_ready, 1)
                if ip == 0 and u >= 2:
                    pe.wait_ge(o_ready, u - 1)
                pe.wait_ge(exp_done, G * (q + 1))
                for k in range(2):
                    i = 2 * ip + k
                    for j in range(G):
                        last = pe.matmul(bank[O_BANK[u % 2]][HEAD_ROWS * j:HEAD_ROWS * (j + 1), 0:TOK],
                                         Va[:, i, G * g + j, :], PT[:, (G * q + j) % NP_RING, k * TOK:(k + 1) * TOK],
                                         start=(i == 0), stop=(i == NI - 1), skip_group_check=True)
                last.then_inc(pv_done, 1)

            def transpose_output(u):
                pe.wait_ge(o_ready, u + 1)
                misc_free()
                for t in range(HT):
                    last = pe.transpose(bank[MISC][:, t * P:(t + 1) * P], O_sb[:, u, t * P:(t + 1) * P], ident[:])
                last.then_inc(oT_done, 1)
                misc_uses.append((onat_ready, u + 1))

            def transpose_normalised(half):
                misc_free()
                for t in range(HT):
                    last = pe.transpose(bank[MISC][:, t * P:(t + 1) * P],
                                        o_nat[:, half, t, :, :].rearrange("p h d -> p (h d)"), ident[:])
                last.then_inc(onatT_done, 1)
                misc_uses.append((onatT_ready, half + 1))

            def project(half):
                misc_free()
                for t in range(HT):
                    last = pe.matmul(bank[MISC][:, t * P:(t + 1) * P], o_natT[:, half, t * P:(t + 1) * P], wT[:, 3, :],
                                     start=True, stop=True)
                last.then_inc(proj_done, 1)
                misc_uses.append((x2_ready, half + 1))

            def transpose_xn2(half):
                pe.wait_ge(xn2_ready, half + 1)
                misc_free()
                for t in range(HT):
                    last = pe.transpose(bank[MISC][:, t * P:(t + 1) * P], xn2[:, half * HT + t, :], ident[:])
                last.then_inc(xn2T_done, 1)
                misc_uses.append((xn2T_ready, half + 1))

            def route(half):
                pe.wait_ge(in_small, 32)
                misc_free()
                for t in range(HT):
                    last = pe.matmul(bank[MISC][:, t * NE:(t + 1) * NE], xn2T[:, half, t * P:(t + 1) * P], wr_sb[:],
                                     start=True, stop=True)
                last.then_inc(logits_done, 1)
                misc_uses.append((logits_used, half + 1))

            def output_bias(half):
                pe.wait_ge(wexp_ready, half + 1)
                misc_free()
                for t in range(HT):
                    last = pe.transpose(bank[MISC][0:NE, t * P:(t + 1) * P], wexp[:, half * HT + t, :], ident[:])
                last.then_inc(wexpT_done, 1)
                pe.wait_ge(wexpT_ready, half + 1)
                for t in range(HT):
                    last = pe.matmul(bank[MISC][:, t * P:(t + 1) * P], wexpT[:, half, t * P:(t + 1) * P], b2_sb[:],
                                     start=True, stop=True)
                last.then_inc(b2_done, 1)
                misc_uses.append((acc0_ready, half + 1))

            def hidden(n):
                half, e, c = n // HALF_E, n % HALF_E // FC, n % FC
                if c == 0:
                    pe.wait_ge(xe_ready, n // FC + 1)
                    pe.wait_ge(w1part_ready, e + 1)
                if n < len(X_BANK):
                    pe.wait_ge(exp_done, NU * NX_U)
                else:
                    pe.wait_ge(hid_ready, n - len(X_BANK) + 1)
                b, z = bank[X_BANK[n % len(X_BANK)]], (n // FC) % 2
                w = w1_part[:, e, :, c * P:(c + 1) * P]
                pe.matmul(b[:, 0:TOK], w[:, 0, :], xe_part[:, z, 0, :], start=True, stop=False)
                pe.matmul(b[:, 0:TOK], w[:, 0, :], xe_part[:, z, 1, :], start=False, stop=False)
                pe.matmul(b[:, 0:TOK], w[:, 1, :], xe_part[:, z, 0, :], start=False, stop=True).then_inc(f1_done, 1)

            def expert_out(n):
                e, c, m = n % HALF_E // FC, n % FC, n // FC
                if n < FC:
                    pe.wait_ge(s_used, NU * NS_U)
                if c == 0:
                    pe.wait_ge(in_w2[e], 16)
                    if m >= 2:
                        pe.wait_ge(y_used, m - 1)
                pe.wait_ge(hid_ready, n + 1)
                for t in range(HT):
                    last = pe.matmul(bank[S_BANK[m % 2]][:, t * P:(t + 1) * P], hid[:, n % NH_RING, t * P:(t + 1) * P],
                                     w2_sb[:, e, c, :], start=(c == 0 and t == 0), stop=(c == FC - 1 and t == HT - 1),
                                     skip_group_check=True)
                last.then_inc(f2_done, 1)

            def transpose_masks(p):
                pe.wait_ge(ident_ready, 2)
                pe.wait_ge(maskb_ready, NT)
                b = bank[(6, 5)[p]][:].bitcast(BF16)
                if p == 1:
                    pe.wait_ge(va_ready, 1)
                for k in range(2):
                    for t in range(NT):
                        i = 2 * p + k
                        last = pe.transpose(b[:, k * T + t * P:k * T + (t + 1) * P], maskb[:, t, i * P:(i + 1) * P], identb[:])
                last.then_inc(mT_done, 1)

            pe.wait_ge(const_ready, 4)
            pe.wait_ge(xn1T_ready, 1)
            for n in range(4):
                pick(n)
                if n % 2:
                    score(2 * (n // 2))
                    score(2 * (n // 2) + 1)
            for n in range(G, NS_U):
                score(n)
                pick(n)
            transpose_masks(0)
            transpose_masks(1)
            transpose_maxima(0)
            for n in range(NS_U, LEAD):
                score(n)
            late = {14: lambda: transpose_output(0), 22: lambda: transpose_output(1), 24: lambda: transpose_normalised(0),
                    25: lambda: project(0), 29: lambda: transpose_xn2(0), 30: lambda: route(0)}
            for n in range(NU * NX_U):
                transposed_scores(n)
                if n + LEAD < NU * NS_U:
                    score(n + LEAD)
                if n % NX_U == 6 and n // NX_U + 1 < NU:
                    transpose_maxima(n // NX_U + 1)
                if n % G == 1 and n >= G + 1:
                    weighted_values(n // G - 1)
                if n in late:
                    late[n]()
            weighted_values(NU * NIP - 1)

            tail = {0: lambda: transpose_output(2), 2: lambda: transpose_output(3), 4: lambda: output_bias(0),
                    6: lambda: transpose_normalised(1), 8: lambda: project(1), 16: lambda: transpose_xn2(1),
                    18: lambda: route(1), 24: lambda: output_bias(1)}
            for n in range(NHALF * HALF_E + FC):
                if n < NHALF * HALF_E:
                    hidden(n)
                if n >= FC:
                    expert_out(n - FC)
                if n in tail:
                    tail[n]()

        @block.scalar
        def _(act):
            steps = [0]
            act.dma_start(hn_sb[:], h_neigh.rearrange("(i p) d -> p i d", p=P)).then_inc(in_hn, 16)
            act.dma_start(rows[R_B1:R_G, :], b1.rearrange("e (c p) -> (e c) p", p=P)).then_inc(in_rows, 16)
            act.dma_start(rows[R_G:R_B, :], ln_g).then_inc(in_rows, 16)
            act.dma_start(rows[R_B:R_BQ, :], ln_b).then_inc(in_rows, 16)
            act.dma_start(rows[R_BQ:R_BK, :], bq.rearrange("(a d) -> a d", a=1)).then_inc(in_rows, 16)
            act.dma_start(rows[R_BK:R_E1, :], bk.rearrange("(a d) -> a d", a=1)).then_inc(in_rows, 16)
            act.dma_start(rows[R_E1:NROWS, :], E[1:2, :]).then_inc(in_rows, 16)
            act.dma_start(w_sb[:, 1, :], Wk).then_inc(in_w, 16)
            act.dma_start(w_sb[:, 2, :], Wv).then_inc(in_w, 16)
            act.dma_start(wo_sb[:], Wo).then_inc(in_wo, 16)
            act.wait_ge(rows_done, 1)
            act.activation(cols[:], bank[MISC][:, 0:NROWS], ACT.Copy).then_inc(cols_ready, 1)
            act.wait_ge(cols_ready, 1)
            act.wait_ge(hT_done, 1)
            act.activation(msgT[:], bank[2][:], ACT.Identity, bias=cols[:, R_E1:R_E1 + 1]).then_inc(msgT_ready, 1)
            act.wait_ge(w_done, 1)
            act.activation(wT[:].rearrange("p a d -> p (a d)"), bank[1][:], ACT.Copy).then_inc(wT_ready, 1)
            act.wait_ge(k_done, 1)
            act.activation(k_full[:], bank[4][:], ACT.Identity, bias=cols[:, R_BK:R_BK + 1]).then_inc(kfull_ready, 1)

            def heads(n):
                pair, what = n // 2, n % 2
                act.wait_ge(picked, n + 1)
                for a in range(2):
                    act.activation((KA, QA)[what][0:MAXROW, 2 * pair + a, :], bank[4 - n % 2][64 * a:64 * (a + 1), :],
                                   ACT.Copy).then_inc(heads_ready, 1)

            for n in range(H):
                heads(n)
            act.wait_ge(mT_done, 1)
            act.activation(maskT[:, 0:2, :].rearrange("p i t -> p (i t)"), bank[6][:].bitcast(BF16), ACT.Copy).then_inc(maskT_ready, 1)

            def maxima(u):
                act.wait_ge(nmaxT_done, u + 1)
                act.activation(nmaxT[:, u, :], bank[MISC][0:PARTS * G, 0:TOK], ACT.Copy).then_inc(nmaxT_ready, 1)

            def exponential(n):
                act.wait_ge(st_done, n + 1)
                if n >= NP_RING:
                    act.wait_ge(pv_done, n // G - 1)
                act.activation(PT[:, n % NP_RING, :], bank[X_BANK[n % len(X_BANK)]][:], ACT.Exp).then_inc(exp_done, 1)

            def output(u):
                act.wait_ge(pv_done, NIP * (u + 1))
                act.activation(O_sb[:, u, :], bank[O_BANK[u % 2]][:, 0:TOK], ACT.Copy).then_inc(o_ready, 1)

            def w1_rounded(e):
                act.wait_ge(in_w1[e], 16)
                act.activation(w1_part[:, e, 0, :], w1_sb[:, e, :], ACT.Copy).then_inc(w1hi_ready, 1)

            def from_misc(done, dst, ready, half, rows_=P):
                act.wait_ge(done, half + 1)
                act.activation(dst, bank[MISC][0:rows_, 0:TOK], ACT.Copy).then_inc(ready, 1)

            maxima(0)
            for n in range(NU * NX_U):
                exponential(n)
                if n % NX_U == 6 and n // NX_U + 1 < NU:
                    maxima(n // NX_U + 1)
                if n % NX_U == 1 and n > NX_U:
                    output(n // NX_U - 1)
                if n % 2 == 0 and 2 <= n < 2 + 2 * NE:
                    w1_rounded(n // 2 - 1)
                if n == 24:
                    from_misc(onatT_done, o_natT[:, 0, :], onatT_ready, 0)
                if n == 29:
                    from_misc(xn2T_done, xn2T[:, 0, :], xn2T_ready, 0)
            output(NU - 1)
            for n in range(NHALF * HALF_E):
                act.wait_ge(f1_done, n + 1)
                if n >= NH_RING:
                    act.wait_ge(f2_done, n - NH_RING + 1)
                act.activation(hid[:, n % NH_RING, :], bank[X_BANK[n % len(X_BANK)]][:, 0:TOK], ACT.Gelu,
                               bias=cols[:, R_B1 + n % HALF_E:R_B1 + n % HALF_E + 1]).then_inc(hid_ready, 1)
                if n == 4:
                    from_misc(wexpT_done, wexpT[:, 0, :], wexpT_ready, 0, NE)
                if n == 7:
                    from_misc(onatT_done, o_natT[:, 1, :], onatT_ready, 1)
                if n == 17:
                    from_misc(xn2T_done, xn2T[:, 1, :], xn2T_ready, 1)
                if n == 24:
                    from_misc(wexpT_done, wexpT[:, 1, :], wexpT_ready, 1, NE)

        @block.vector
        def _(dve):
            steps = [0]

            def step(ins):
                steps[0] += 1
                ins.then_inc(dve_step, 1)
                dve.wait_ge(dve_step, steps[0])

            dve.wait_ge(ident_ready, 1)
            dve.wait_ge(pick_zero, 2)
            head_rows = ident[:].rearrange("p (h d) -> p h d", d=DH).unsqueeze(2).broadcast_to([P, H, 2, DH])
            for part in range(PARTS):
                q_cols = pick_q[:, part, :, :].rearrange("p h (c r d) -> p h c r d", c=2, d=DH)[:, :, part, :, :]
                k_cols = pick_k[:, part, :, :].rearrange("p h (r c d) -> p h r c d", c=2, d=DH)[:, :, :, part, :]
                dve.tensor_copy(q_cols, head_rows).then_inc(pick_ready, 1)
                dve.tensor_copy(k_cols, head_rows).then_inc(pick_ready, 1)
            dve.wait_ge(in_x, 16)
            for t in range(NT):
                last = dve.bn_stats(stats[:, t, :], x_sb[:, t, :])
            step(last)
            for t in range(NT):
                last = dve.bn_aggr(mv[:, t, :], stats[:, t, :])
            step(last)
            dve.tensor_scalar(var_eps[:], mv[:, :, 1], EPS, None, ALU.add).then_inc(var1_ready, 1)
            dve.wait_ge(rstd1_ready, 1)
            for t in range(NT):
                last = dve.tensor_scalar(xn1[:, t, :], x_sb[:, t, :], mv[:, t, 0:1], rstd[:, t:t + 1], ALU.subtract, ALU.mult)
            last.then_inc(xn1_ready, 1)
            dve.wait_ge(kfull_ready, 1)
            step(dve.tensor_copy(k_part[:, 0, :], k_full[:]))
            dve.tensor_tensor(k_part[:, 1, :], k_full[:], k_part[:, 0, :].bitcast(F32), ALU.subtract).then_inc(kpart_ready, 1)
            dve.wait_ge(xT_done, 1)
            dve.tensor_copy(xn1T[:], bank[0][:]).then_inc(xn1T_ready, 1)
            dve.wait_ge(q_done, 1)
            dve.wait_ge(cols_ready, 1)
            step(dve.tensor_scalar(q_full[:], bank[3][:], cols[:, R_BQ:R_BQ + 1], float(DH) ** -0.5, ALU.add, ALU.mult))
            step(dve.tensor_copy(q_part[:, 0, :], q_full[:]))
            dve.tensor_tensor(q_part[:, 1, :], q_full[:], q_part[:, 0, :].bitcast(F32), ALU.subtract).then_inc(qpart_ready, 1)
            for t in range(NT):
                dve.wait_ge(in_adj, 16 * NT)
                dve.tensor_scalar(maskb[:, t, :], adj_sb[:, t, :], 0.0, MASKED, ALU.is_equal, ALU.mult).then_inc(maskb_ready, 1)
            dve.wait_ge(v_done, 1)
            dve.wait_ge(in_bc, 48)
            dve.wait_ge(const_ready, 2)
            for i in range(NI):
                last = dve.tensor_tensor(Va[:, i, :, 0:DH], bank[5][:, i * P:(i + 1) * P].rearrange("p (h d) -> p h d", d=DH),
                                         bv_bc[:].rearrange("p (h d) -> p h d", d=DH), ALU.add)
            last.then_inc(va_ready, 1)

            def maximum(n):
                u, r = n // NS_U, n % NS_U
                if n == 0:
                    dve.wait_ge(maskb_ready, NT)
                dve.wait_ge(s_done, n + 1)
                dve.tensor_tensor_reduce(out=junk[:, n % 2, :], in0=bank[S_BANK[n % 2]][:],
                                         in1=maskb[:, unit[u][0] * HT + r // G, :], scale=1.0, scalar=-3e38,
                                         op0=ALU.add, op1=ALU.max, accum_out=mx[:, u, r:r + 1]).then_inc(s_used, 1)

            def negative_maxima(u):
                dve.wait_ge(s_used, NS_U * (u + 1))
                nm = nmax[:, u, :].rearrange("p (t j) -> p t j", j=G)
                step(dve.tensor_scalar(nmax[:, u, :], mx[:, u, :], LOWEST_MAX, -1.0, ALU.max, ALU.mult))
                step(dve.tensor_copy(nmax_part[:, u, :, 0, :], nm))
                dve.tensor_tensor(nmax_part[:, u, :, 1, :], nm, nmax_part[:, u, :, 0, :].bitcast(F32),
                                  ALU.subtract).then_inc(nmax_ready, 1)

            def normalise(u):
                half, g = unit[u]
                dve.wait_ge(oT_done, u + 1)
                o = bank[MISC][:, 0:TOK].rearrange("p (t j r) -> p t j r", t=HT, j=G)
                d = den[:, u, :].rearrange("p (t j) -> p t j", j=G)
                step(dve.tensor_scalar(d, o[:, :, :, DH], TINY, None, ALU.max))
                step(dve.reciprocal(rden[:, u, :], den[:, u, :]))
                for t in range(HT):
                    r = rden[:, u, t * G:(t + 1) * G].unsqueeze(2).broadcast_to([P, G, DH])
                    last = dve.tensor_tensor(o_nat[:, half, t, G * g:G * g + G, :], o[:, t, :, 0:DH], r, ALU.mult)
                last.then_inc(onat_ready, 1)

            def second_norms(half):
                ts = slice(half * HT, (half + 1) * HT)
                dve.wait_ge(proj_done, half + 1)
                dve.wait_ge(xb_ready, 1)
                dve.tensor_tensor(x2[:, ts, :], bank[MISC][:, 0:TOK].rearrange("p (t d) -> p t d", d=D), xb[:, ts, :],
                                  ALU.add).then_inc(x2_ready, 1)
                dve.wait_ge(x2_ready, half + 1)
                for t in range(half * HT, (half + 1) * HT):
                    last = dve.bn_stats(stats2[:, t, :], x2[:, t, :])
                step(last)
                for t in range(half * HT, (half + 1) * HT):
                    last = dve.bn_aggr(mv2[:, t, :], stats2[:, t, :])
                step(last)
                dve.tensor_scalar(va[:, ts], mv2[:, ts, 1], EPS, None, ALU.add).then_inc(va2_ready, 1)

            def second_norms_b(half):
                ts = slice(half * HT, (half + 1) * HT)
                dve.wait_ge(ra_ready, half + 1)
                step(dve.tensor_tensor(ra2[:, ts], ra[:, ts], ra[:, ts], ALU.mult))
                step(dve.tensor_tensor(vb[:, ts], ra2[:, ts], mv2[:, ts, 1], ALU.mult))
                dve.tensor_scalar(vb[:, ts], vb[:, ts], EPS, None, ALU.add).then_inc(vb_ready, 1)

            def second_norms_c(half):
                ts = slice(half * HT, (half + 1) * HT)
                dve.wait_ge(rb_ready, half + 1)
                step(dve.tensor_tensor(rab[:, ts], ra[:, ts], rb[:, ts], ALU.mult))
                dve.tensor_tensor(sdb[:, ts], vb[:, ts], rb[:, ts], ALU.mult)
                for t in range(half * HT, (half + 1) * HT):
                    last = dve.tensor_scalar(xn2[:, t, :], x2[:, t, :], mv2[:, t, 0:1], rab[:, t:t + 1], ALU.subtract, ALU.mult)
                last.then_inc(xn2_ready, 1)

            def router(half):
                ts, tiles = slice(half * HT, (half + 1) * HT), range(half * HT, (half + 1) * HT)
                dve.wait_ge(logits_done, half + 1)
                for t in tiles:
                    k = t - half * HT
                    last = dve.scalar_tensor_tensor(out=logits[:, t, :], in0=bank[MISC][:, k * NE:(k + 1) * NE],
                                                    scalar=sdb[:, t:t + 1], in1=br_bc[:], op0=ALU.mult, op1=ALU.add)
                last.then_inc(logits_used, 1)
                dve.wait_ge(logits_used, half + 1)
                for t in tiles:
                    last = dve.max(top[:, t, :], logits[:, t, :])
                step(last)
                dve.tensor_tensor(gap[:, ts], top[:, ts, 1], top[:, ts, 0], ALU.subtract).then_inc(gap_ready, 1)
                for t in tiles:
                    last = dve.max_index(top_at[:, t, :], top[:, t, :], logits[:, t, :])
                step(last)
                dve.tensor_copy(top_no[:, ts, :], top_at[:, ts, 0:2])

            def router_b(half):
                ts, tiles = slice(half * HT, (half + 1) * HT), range(half * HT, (half + 1) * HT)
                dve.wait_ge(egap_ready, half + 1)
                step(dve.tensor_scalar(dgap[:, ts], egap[:, ts], 1.0, None, ALU.add))
                step(dve.reciprocal(wtop[:, ts, 0], dgap[:, ts]))
                step(dve.tensor_tensor(wtop[:, ts, 1], wtop[:, ts, 0], egap[:, ts], ALU.mult))
                dve.wait_ge(const_ready, 5)
                for t in tiles:
                    dve.tensor_scalar(wfirst[:, t, :], expert_no[:], top_no[:, t, 0:1], wtop[:, t, 0:1], ALU.is_equal, ALU.mult)
                    last = dve.tensor_scalar(wsecond[:, t, :], expert_no[:], top_no[:, t, 1:2], wtop[:, t, 1:2], ALU.is_equal, ALU.mult)
                step(last)
                dve.tensor_tensor(wexp[:, ts, :], wfirst[:, ts, :], wsecond[:, ts, :], ALU.add).then_inc(wexp_ready, 1)

            def start_sum(half):
                ts = slice(half * HT, (half + 1) * HT)
                dve.wait_ge(b2_done, half + 1)
                dve.tensor_tensor(acc[:, 1, ts, :], bank[MISC][:, 0:TOK].rearrange("p (t d) -> p t d", d=D), x2[:, ts, :],
                                  ALU.add).then_inc(acc0_ready, 1)
                dve.wait_ge(acc0_ready, half + 1)

            def expert_in(m):
                half, e = m // NE, m % NE
                if e == 0:
                    dve.wait_ge(xn2T_ready, half + 1)
                if m >= 2:
                    dve.wait_ge(f1_done, FC * (m - 1))
                z = m % 2
                step(dve.tensor_scalar(xe[:, z, :], xn2T[:, half, :], cols[:, R_G + e:R_G + e + 1], cols[:, R_B + e:R_B + e + 1],
                                       ALU.mult, ALU.add))
                step(dve.tensor_copy(xe_part[:, z, 0, :], xe[:, z, :]))
                dve.tensor_tensor(xe_part[:, z, 1, :], xe[:, z, :], xe_part[:, z, 0, :].bitcast(F32), ALU.subtract).then_inc(xe_ready, 1)

            def add_expert(m):
                half, e = m // NE, m % NE
                if e == 0:
                    dve.wait_ge(wexp_ready, half + 1)
                dve.wait_ge(f2_done, FC * (m + 1))
                for k in range(HT):
                    t = half * HT + k
                    last = dve.scalar_tensor_tensor(out=acc[:, e % 2, t, :], in0=bank[S_BANK[m % 2]][:, k * P:(k + 1) * P],
                                                    scalar=wexp[:, t, e:e + 1], in1=acc[:, 1 - e % 2, t, :],
                                                    op0=ALU.mult, op1=ALU.add)
                last.then_inc(y_used, 1)
                dve.wait_ge(y_used, m + 1)

            for n in range(NU * NS_U):
                maximum(n)
                if n % NS_U == NS_U - 1:
                    negative_maxima(n // NS_U)
                if n == NS_U - 1:
                    dve.wait_ge(mT_done, 2)
                    dve.tensor_copy(maskT[:, 2:4, :].rearrange("p i t -> p (i t)"), bank[5][:].bitcast(BF16)).then_inc(maskT_ready, 1)
                if n == LEAD + 14:
                    normalise(0)
            normalise(1)
            second_norms(0)
            second_norms_b(0)
            second_norms_c(0)
            expert_in(0)
            router(0)
            router_b(0)
            expert_in(1)
            normalise(2)
            normalise(3)
            start_sum(0)
            for m in range(NHALF * NE):
                add_expert(m)
                if m + 2 < NHALF * NE:
                    expert_in(m + 2)
                if m == 0:
                    second_norms(1)
                if m == 1:
                    second_norms_b(1)
                if m == 2:
                    second_norms_c(1)
                if m == 3:
                    router(1)
                if m == 4:
                    router_b(1)
                if m == 5:
                    start_sum(1)


_INS = ['x', 'adj', 'L0_gnn_h_neigh', 'L0_gnn_Wq', 'L0_gnn_bq', 'L0_gnn_Wk', 'L0_gnn_bk', 'L0_gnn_Wv', 'L0_gnn_bv',
        'L0_gnn_Wo', 'L0_gnn_bo', 'L0_gnn_E', 'L0_ffn_Wr', 'L0_ffn_br', 'L0_ffn_ln_g', 'L0_ffn_ln_b', 'L0_ffn_W1',
        'L0_ffn_b1', 'L0_ffn_W2', 'L0_ffn_b2']
_OUTS = [((512, 128), 'float32')]


def kernel(**inputs):
    import numpy as _np
    import concourse.bacc as _bacc
    from concourse import mybir as _mybir
    from concourse.bass_utils import run_bass_kernel_spmd as _run

    nc = _bacc.Bacc("TRN2", target_bir_lowering=False, num_devices=1)
    arrays, args = {}, []
    for name in _INS:
        a = _np.ascontiguousarray(inputs[name])
        arrays[f"in_{name}_dram"] = a
        args.append(nc.dram_tensor(f"in_{name}_dram", a.shape, _mybir.dt.from_np(a.dtype), kind="ExternalInput").ap())
    for i, (shape, dtype) in enumerate(_OUTS):
        dt = _mybir.dt.from_np(_np.dtype(dtype))
        args.append(nc.dram_tensor(f"out_{i}_dram", shape, dt, kind="ExternalOutput").ap())
    gnn_ffn_kernel(nc, *args)
    r = _run(nc, [arrays], core_ids=[0])
    got = tuple(r.results[0][f"out_{i}_dram"] for i in range(len(_OUTS)))
    return got[0]
```

```python
from contextlib import ExitStack

import concourse.bass as bass
from concourse import mybir

ALU = mybir.AluOpType
ACT = mybir.ActivationFunctionType
F32 = mybir.dt.float32
F32R = mybir.dt.float32r
BF16 = mybir.dt.bfloat16
I32 = mybir.dt.int32
U32 = mybir.dt.uint32

P = 128
EPS = 1e-5
MASKED = -1e9
LOWEST_MAX = -1e8
TINY = 1e-30
HEAD_ROWS = 32
PARTS = 2


def gnn_ffn_kernel(nc, x, adj, h_neigh, Wq, bq, Wk, bk, Wv, bv, Wo, bo, E, Wr, br, ln_g, ln_b, W1, b1, W2, b2, out):
    T, D = x.shape
    N = h_neigh.shape[0]
    NE, _, F = W1.shape
    NT, NI, FC = T // P, N // P, F // P
    DH = 16
    H = D // DH
    G = 4
    NG = H // G
    HT = 2
    NHALF = NT // HT
    TOK = HT * P
    NU = NHALF * NG
    KROWS = 96
    MAXROW = 4 * DH
    assert D == P and N == 512 and T == 512 and H == 8

    NS_U = HT * G
    NIP = NI // 2
    NX_U = NIP * G
    LEAD = NS_U + 6
    NP_RING = 2 * G
    NH_RING = 8
    HALF_E = NE * FC

    C_E1, C_BK, C_BQ, NEARLY = 0, 1, 2, 3
    C_B1, C_G, C_B = NEARLY, NEARLY + NE * FC, NEARLY + NE * FC + NE
    NROWS = NE * FC + 2 * NE

    with ExitStack() as ctx:
        def sb(name, shape, dt):
            return ctx.enter_context(nc.sbuf_tensor(name, shape, dt))

        def sem(name):
            return ctx.enter_context(nc.semaphore(name))

        bank = [ctx.enter_context(nc.psum_tensor(f"bank{i}", [P, 512], F32)) for i in range(8)]
        S_BANK, X_BANK, O_BANK, MISC = [0, 1], [2, 3, 4], [5, 6], 7

        x_sb = sb("x_sb", [P, NT, D], F32)
        adj_sb = sb("adj_sb", [P, NT, N], I32)
        hn_sb = sb("hn_sb", [P, NI, D], F32)
        w_sb = sb("w_sb", [P, 3, D], F32)
        wo_sb = sb("wo_sb", [P, D], F32)
        rows_early = sb("rows_early", [NEARLY, D], F32)
        rows = sb("rows", [NROWS, D], F32)
        bv_bc = sb("bv_bc", [P, D], F32)
        bo_bc = sb("bo_bc", [P, D], F32)
        br_bc = sb("br_bc", [P, NE], F32)
        wr_sb = sb("wr_sb", [P, NE], F32)
        b2_sb = sb("b2_sb", [NE, D], F32)
        w1_sb = sb("w1_sb", [P, NE, F], F32)
        w2_sb = sb("w2_sb", [P, NE, FC, D], F32)
        ident = sb("ident", [P, P], F32)
        identb = sb("identb", [P, P], BF16)
        pick_q = sb("pick_q", [P, PARTS, H, MAXROW], F32R)
        pick_k = sb("pick_k", [P, PARTS, H, MAXROW], F32R)
        half_pow = sb("half_pow", [P, NT], F32)
        euler = sb("euler", [P, HT], F32)
        expert_no = sb("expert_no", [P, NE], F32)
        stats = sb("stats", [P, NT, 6], F32)
        mv = sb("mv", [P, NT, 2], F32)
        var_eps = sb("var_eps", [P, NT], F32)
        rstd = sb("rstd", [P, NT], F32)
        xn1 = sb("xn1", [P, NT, D], F32)
        xb = sb("xb", [P, NT, D], F32)
        xn1T = sb("xn1T", [P, T], F32)
        wT = sb("wT", [P, 4, D], F32)
        cols = sb("cols", [P, NEARLY + NROWS], F32)
        msgT = sb("msgT", [P, N], F32)
        q_full = sb("q_full", [P, T], F32)
        k_full = sb("k_full", [P, N], F32)
        q_part = sb("q_part", [P, PARTS, T], F32R)
        k_part = sb("k_part", [P, PARTS, N], F32R)
        QA = sb("QA", [KROWS, H, T], F32R)
        KA = sb("KA", [KROWS, H, N], F32R)
        Va = sb("Va", [P, NI, H, HEAD_ROWS], F32)
        maskb = sb("maskb", [P, NT, N], BF16)
        maskT = sb("maskT", [P, NI, T], BF16)
        junk = sb("junk", [P, 2, N], BF16)
        mx = sb("mx", [P, NU, NS_U], F32)
        nmax = sb("nmax", [P, NU, NS_U], F32)
        nmax_part = sb("nmax_part", [P, NU, HT, PARTS, G], F32R)
        nmaxT = sb("nmaxT", [PARTS * G, NU, TOK], F32)
        PT = sb("PT", [P, NP_RING, 512], F32)
        O_sb = sb("O_sb", [P, NU, TOK], F32)
        den = sb("den", [P, NU, HT * G], F32)
        rden = sb("rden", [P, NU, HT * G], F32)
        o_nat = sb("o_nat", [P, NHALF, HT, H, DH], F32)
        o_natT = sb("o_natT", [P, NHALF, TOK], F32)
        x2 = sb("x2", [P, NT, D], F32)
        stats2 = sb("stats2", [P, NT, 6], F32)
        mv2 = sb("mv2", [P, NT, 2], F32)
        vw = sb("vw", [P, NT, 2], F32)
        rvw = sb("rvw", [P, NT, 2], F32)
        sw = sb("sw", [P, NT], F32)
        sdb = sb("sdb", [P, NT], F32)
        xn2 = sb("xn2", [P, NT, D], F32)
        xn2T = sb("xn2T", [P, NHALF, TOK], F32)
        logits = sb("logits", [P, NT, NE], F32)
        top = sb("top", [P, NT, 8], F32)
        top_at = sb("top_at", [P, NT, 8], U32)
        top_no = sb("top_no", [P, NT, 2], F32)
        gap = sb("gap", [P, NT], F32)
        egap = sb("egap", [P, NT], F32)
        dgap = sb("dgap", [P, NT], F32)
        wtop = sb("wtop", [P, NT, 2], F32)
        wfirst = sb("wfirst", [P, NT, NE], F32)
        wsecond = sb("wsecond", [P, NT, NE], F32)
        wexp = sb("wexp", [P, NT, NE], F32)
        wexpT = sb("wexpT", [NE, NHALF, TOK], F32)
        w1_part = sb("w1_part", [P, NE, PARTS, F], F32R)
        xe = sb("xe", [P, 2, TOK], F32)
        xe_part = sb("xe_part", [P, 2, PARTS, TOK], F32R)
        hid = PT[:, :, 0:TOK]
        acc = sb("acc", [P, 2, NT, D], F32)

        in_x, in_hn, in_w, in_wo, in_rows, in_bc, in_adj = (sem(n) for n in ("in_x", "in_hn", "in_w", "in_wo", "in_rows", "in_bc", "in_adj"))
        in_early, cols_early_ready, early_done = sem("in_early"), sem("cols_early_ready"), sem("early_done")
        in_small, in_w1, in_w2 = sem("in_small"), [sem(f"in_w1_{e}") for e in range(NE)], [sem(f"in_w2_{e}") for e in range(NE)]
        ident_ready, pick_zero, pick_ready, const_ready, pool_step = sem("ident_ready"), sem("pick_zero"), sem("pick_ready"), sem("const_ready"), sem("pool_step")
        dve_step, act_step = sem("dve_step"), sem("act_step")
        var1_ready, rstd1_ready, xn1_ready, xn1T_ready = sem("var1_ready"), sem("rstd1_ready"), sem("xn1_ready"), sem("xn1T_ready")
        xT_done, w_done, hT_done, rows_done, wo_done, q_done, k_done, v_done, mT_done = (
            sem(n) for n in ("xT_done", "w_done", "hT_done", "rows_done", "wo_done", "q_done", "k_done", "v_done", "mT_done"))
        wT_ready, cols_ready, msgT_ready, kfull_ready, qpart_ready, kpart_ready = (
            sem(n) for n in ("wT_ready", "cols_ready", "msgT_ready", "kfull_ready", "qpart_ready", "kpart_ready"))
        va_ready, maskb_ready, maskT_ready, woT_ready, xb_ready = (
            sem(n) for n in ("va_ready", "maskb_ready", "maskT_ready", "woT_ready", "xb_ready"))
        picked, heads_ready = sem("picked"), sem("heads_ready")
        s_done, s_used = sem("s_done"), sem("s_used")
        nmax_ready, nmaxT_done, nmaxT_ready, nmax_in = sem("nmax_ready"), sem("nmaxT_done"), sem("nmaxT_ready"), sem("nmax_in")
        st_done, exp_done, pv_done, o_ready = sem("st_done"), sem("exp_done"), sem("pv_done"), sem("o_ready")
        oT_done, onat_ready, onatT_done, onatT_ready, proj_done, x2_ready = (
            sem(n) for n in ("oT_done", "onat_ready", "onatT_done", "onatT_ready", "proj_done", "x2_ready"))
        vw_ready, rvw_ready, xn2_ready, xn2T_done, xn2T_ready = (
            sem(n) for n in ("vw_ready", "rvw_ready", "xn2_ready", "xn2T_done", "xn2T_ready"))
        logits_done, gap_ready, egap_ready, wexp_ready, wexpT_done, wexpT_ready, b2_done, acc0_ready, logits_used = (
            sem(n) for n in ("logits_done", "gap_ready", "egap_ready", "wexp_ready", "wexpT_done", "wexpT_ready", "b2_done", "acc0_ready", "logits_used"))
        oT_used = sem("oT_used")
        w1hi_ready, w1part_ready, xe_ready, f1_done, hid_ready, f2_done, y_used, stored = (
            sem(n) for n in ("w1hi_ready", "w1part_ready", "xe_ready", "f1_done", "hid_ready", "f2_done", "y_used", "stored"))

        block = ctx.enter_context(nc.Block())

        unit = [(half, g) for half in range(NHALF) for g in range(NG)]
        picks = [(what, pair) for g in range(NG) for what in (0, 1) for pair in (2 * g, 2 * g + 1)]
        PICK_BANK = [4, 6, 3]

        def tile_of(r):
            return r // 2 % HT, 2 * (r // (2 * HT)) + r % 2

        @block.sync
        def _(sp):
            sp.dma_start(x_sb[:], x.rearrange("(t p) d -> p t d", p=P)).then_inc(in_x, 16)
            sp.dma_start(w_sb[:, 1, :], Wk).then_inc(in_w, 16)
            sp.dma_start(w_sb[:, 0, :], Wq).then_inc(in_w, 16)
            sp.dma_start(adj_sb[:], adj.rearrange("(t p) n -> p t n", p=P)).then_inc(in_adj, 16)
            sp.dma_start(w_sb[:, 2, :], Wv).then_inc(in_w, 16)
            sp.dma_start(wo_sb[:], Wo).then_inc(in_wo, 16)
            for e in range(NE):
                sp.dma_start(w1_sb[:, e, :], W1[e]).then_inc(in_w1[e], 16)
            for u, (half, g) in enumerate(unit):
                sp.wait_ge(nmaxT_ready, u + 1)
                sp.dma_start(QA[MAXROW:MAXROW + PARTS, G * g:G * g + G, half * TOK:(half + 1) * TOK].bitcast(F32),
                             nmaxT[:, u, :]).then_inc(nmax_in, 16)
                if u < NE // 2:
                    for e in (2 * u, 2 * u + 1):
                        sp.dma_start(w2_sb[:, e, :, :], W2[e].rearrange("(c p) d -> p c d", p=P)).then_inc(in_w2[e], 16)
            for half in range(NHALF):
                sp.wait_ge(y_used, NE * (half + 1))
                sp.dma_start(out[half * TOK:(half + 1) * TOK, :].rearrange("(t p) d -> p t d", p=P),
                             acc[:, (NE - 1) % 2, half * HT:(half + 1) * HT, :]).then_inc(stored, 16)
            sp.wait_ge(stored, 16 * NHALF)

        @block.gpsimd
        def _(pool):
            steps = [0]

            def step(ins):
                steps[0] += 1
                ins.then_inc(pool_step, 1)
                pool.wait_ge(pool_step, steps[0])

            step(pool.memset(ident[:], 0.0))
            pool.affine_select(out=ident[:], in_=ident[:], compare_op=ALU.not_equal, fill=1.0, base=0,
                               pattern=[[-1, P]], channel_multiplier=1).then_inc(ident_ready, 1)
            for c, row in ((C_E1, E[1:2, :]), (C_BK, bk.rearrange("(a d) -> a d", a=1)), (C_BQ, bq.rearrange("(a d) -> a d", a=1))):
                pool.dma_start(rows_early[c:c + 1, :], row).then_inc(in_early, 16)
            pool.memset(half_pow[:], -0.5)
            pool.memset(euler[:], 2.718281828459045)
            step(pool.memset(identb[:], 0.0))
            pool.affine_select(out=identb[:], in_=identb[:], compare_op=ALU.not_equal, fill=1.0, base=0,
                               pattern=[[-1, P]], channel_multiplier=1).then_inc(ident_ready, 1)
            pool.wait_ge(ident_ready, 2)
            pool.memset(KA[MAXROW:KROWS, :, :].bitcast(F32), 1.0).then_inc(const_ready, 1)
            pool.wait_ge(const_ready, 1)
            pool.wait_ge(var1_ready, 1)
            pool.tensor_tensor(rstd[:], var_eps[:], half_pow[:], ALU.pow).then_inc(rstd1_ready, 1)
            pool.wait_ge(rstd1_ready, 1)
            pool.memset(QA[MAXROW:KROWS, :, :].bitcast(F32), 0.0).then_inc(const_ready, 1)
            pool.wait_ge(const_ready, 2)
            pool.dma_start(bv_bc[:], bv.partition_broadcast(P)).then_inc(in_bc, 16)
            pool.dma_start(bo_bc[:], bo.partition_broadcast(P)).then_inc(in_bc, 16)
            pool.dma_start(br_bc[:], br.partition_broadcast(P)).then_inc(in_bc, 16)
            pool.dma_start(rows[0:NE * FC, :], b1.rearrange("e (c p) -> (e c) p", p=P)).then_inc(in_rows, 16)
            pool.dma_start(rows[NE * FC:NE * FC + NE, :], ln_g).then_inc(in_rows, 16)
            pool.dma_start(rows[NE * FC + NE:NROWS, :], ln_b).then_inc(in_rows, 16)
            pool.dma_start(wr_sb[:], Wr).then_inc(in_small, 16)
            pool.dma_start(b2_sb[:], b2).then_inc(in_small, 16)
            pool.memset(Va[:], 0.0).then_inc(const_ready, 1)
            pool.wait_ge(const_ready, 3)
            pool.memset(Va[:, :, :, DH:DH + 1], 1.0).then_inc(const_ready, 1)
            pool.wait_ge(const_ready, 4)
            pool.iota(expert_no[:], pattern=[[1, NE]], base=0, channel_multiplier=0,
                      allow_small_or_imprecise_dtypes=True).then_inc(const_ready, 1)
            pool.wait_ge(in_x, 16)
            pool.wait_ge(in_bc, 48)
            for t in range(NT):
                last = pool.tensor_tensor(xb[:, t, :], x_sb[:, t, :], bo_bc[:], ALU.add)
            last.then_inc(xb_ready, 1)
            def w1_rest(e):
                pool.wait_ge(w1hi_ready, e + 1)
                pool.tensor_tensor(w1_part[:, e, 1, :], w1_sb[:, e, :], w1_part[:, e, 0, :].bitcast(F32),
                                   ALU.subtract).then_inc(w1part_ready, 1)

            for e in range(NE // 2):
                w1_rest(e)
            for half in range(NHALF):
                ts = slice(half * HT, (half + 1) * HT)
                pool.wait_ge(vw_ready, half + 1)
                pool.tensor_tensor(rvw[:, ts, :].rearrange("p t k -> p (t k)"), vw[:, ts, :].rearrange("p t k -> p (t k)"),
                                   half_pow[:], ALU.pow).then_inc(rvw_ready, 1)
                pool.wait_ge(gap_ready, half + 1)
                pool.tensor_tensor(egap[:, ts], euler[:], gap[:, ts], ALU.pow).then_inc(egap_ready, 1)
                if half == 0:
                    for e in range(NE // 2, NE):
                        w1_rest(e)

        @block.tensor
        def _(pe):
            misc_uses = [(cols_early_ready, 1)]

            pe.wait_ge(ident_ready, 1)
            pe.wait_ge(in_hn, 16)
            for i in range(NI):
                last = pe.transpose(bank[2][:, i * P:(i + 1) * P], hn_sb[:, i, :], ident[:])
            last.then_inc(hT_done, 1)
            pe.wait_ge(in_early, 16 * NEARLY)
            pe.transpose(bank[MISC][:, 0:NEARLY], rows_early[:], ident[0:NEARLY, 0:NEARLY]).then_inc(early_done, 1)
            pe.wait_ge(in_w, 48)
            for k in range(3):
                pe.transpose(bank[1][:, k * P:(k + 1) * P], w_sb[:, k, :], ident[:])
            pe.wait_ge(in_wo, 16)
            pe.transpose(bank[1][:, 3 * P:4 * P], wo_sb[:], ident[:]).then_inc(w_done, 1)
            pe.wait_ge(xn1_ready, 1)
            for t in range(NT):
                last = pe.transpose(bank[0][:, t * P:(t + 1) * P], xn1[:, t, :], ident[:])
            last.then_inc(xT_done, 1)
            pe.wait_ge(wT_ready, 1)
            pe.wait_ge(msgT_ready, 1)
            pe.matmul(bank[4][:], wT[:, 1, :], msgT[:], start=True, stop=True).then_inc(k_done, 1)
            pe.wait_ge(xn1T_ready, 1)
            pe.matmul(bank[3][:], wT[:, 0, :], xn1T[:], start=True, stop=True).then_inc(q_done, 1)
            for i in range(NI):
                last = pe.matmul(bank[5][:, i * P:(i + 1) * P], msgT[:, i * P:(i + 1) * P], wT[:, 2, :], start=True, stop=True)
            last.then_inc(v_done, 1)

            def pick(n):
                what, pair = picks[n]
                src, pick_w, part_ready = ((k_part, pick_k, kpart_ready), (q_part, pick_q, qpart_ready))[what]
                pe.wait_ge(part_ready, 1)
                pe.wait_ge(pick_ready, 2 * PARTS)
                if n >= len(PICK_BANK):
                    pe.wait_ge(heads_ready, 2 * (n - len(PICK_BANK) + 1))
                b = bank[PICK_BANK[n % len(PICK_BANK)]]
                for part in range(PARTS):
                    last = pe.matmul(b[:], pick_w[:, part, 2 * pair:2 * pair + 2, :].rearrange("p a r -> p (a r)"),
                                     src[:, part, :], start=(part == 0), stop=(part == PARTS - 1))
                last.then_inc(picked, 1)

            def score(n):
                u, r = n // NS_U, n % NS_U
                half, g = unit[u]
                t, j = tile_of(r)
                t += half * HT
                if t == 0:
                    pe.wait_ge(heads_ready, 2 * picks.index((1, (G * g + j) // 2)) + 1 + j % 2)
                if n >= 2:
                    pe.wait_ge(s_used, n - 1)
                pe.matmul(bank[S_BANK[n % 2]][:], QA[:, G * g + j, t * P:(t + 1) * P], KA[:, G * g + j, :],
                          start=True, stop=True).then_inc(s_done, 1)

            def transpose_maxima(u):
                pe.wait_ge(nmax_ready, u + 1)
                misc_free()
                for t in range(HT):
                    last = pe.transpose(bank[MISC][0:PARTS * G, t * P:(t + 1) * P],
                                        nmax_part[:, u, t, :, :].bitcast(F32).rearrange("p a b -> p (a b)"), ident[:])
                last.then_inc(nmaxT_done, 1)
                misc_uses.append((nmaxT_ready, u + 1))

            def misc_free():
                if misc_uses:
                    pe.wait_ge(*misc_uses[-1])

            def transposed_scores(n):
                u, r = n // NX_U, n % NX_U
                half, g = unit[u]
                ip, head = r // G, G * g + r % G
                if r == 0:
                    pe.wait_ge(nmax_in, 16 * (u + 1))
                if n == 0:
                    pe.wait_ge(maskT_ready, 2)
                    pe.wait_ge(heads_ready, 2 * H)
                if n >= len(X_BANK):
                    pe.wait_ge(exp_done, n - len(X_BANK) + 1)
                b = bank[X_BANK[n % len(X_BANK)]]
                pe.matmul(b[:], identb[:], maskT[:, 2 * ip:2 * ip + 2, half * TOK:(half + 1) * TOK], start=True, stop=False)
                for k in range(2):
                    i = 2 * ip + k
                    last = pe.matmul(b[:, k * TOK:(k + 1) * TOK], KA[:, head, i * P:(i + 1) * P],
                                     QA[:, head, half * TOK:(half + 1) * TOK], start=False, stop=(k == 1))
                last.then_inc(st_done, 1)

            def weighted_values(q):
                u, ip = q // NIP, q % NIP
                half, g = unit[u]
                if q == 0:
                    pe.wait_ge(va_ready, 1)
                if ip == 0 and u >= 2:
                    pe.wait_ge(o_ready, u - 1)
                pe.wait_ge(exp_done, G * (q + 1))
                for k in range(2):
                    i = 2 * ip + k
                    for j in range(G):
                        last = pe.matmul(bank[O_BANK[u % 2]][HEAD_ROWS * j:HEAD_ROWS * (j + 1), 0:TOK],
                                         Va[:, i, G * g + j, :], PT[:, (G * q + j) % NP_RING, k * TOK:(k + 1) * TOK],
                                         start=(i == 0), stop=(i == NI - 1), skip_group_check=True)
                last.then_inc(pv_done, 1)

            def transpose_output(u):
                pe.wait_ge(o_ready, u + 1)
                misc_free()
                for t in range(HT):
                    last = pe.transpose(bank[MISC][:, t * P:(t + 1) * P], O_sb[:, u, t * P:(t + 1) * P], ident[:])
                last.then_inc(oT_done, 1)
                misc_uses.append((onat_ready, u + 1))

            def transpose_normalised(half):
                misc_free()
                for t in range(HT):
                    last = pe.transpose(bank[MISC][:, t * P:(t + 1) * P],
                                        o_nat[:, half, t, :, :].rearrange("p h d -> p (h d)"), ident[:])
                last.then_inc(onatT_done, 1)
                misc_uses.append((onatT_ready, half + 1))

            def project(half):
                misc_free()
                for t in range(HT):
                    last = pe.matmul(bank[MISC][:, t * P:(t + 1) * P], o_natT[:, half, t * P:(t + 1) * P], wT[:, 3, :],
                                     start=True, stop=True)
                last.then_inc(proj_done, 1)
                misc_uses.append((x2_ready, half + 1))

            def transpose_xn2(half):
                pe.wait_ge(xn2_ready, half + 1)
                misc_free()
                for t in range(HT):
                    last = pe.transpose(bank[MISC][:, t * P:(t + 1) * P], xn2[:, half * HT + t, :], ident[:])
                last.then_inc(xn2T_done, 1)
                misc_uses.append((xn2T_ready, half + 1))

            def route(half):
                pe.wait_ge(in_small, 32)
                misc_free()
                for t in range(HT):
                    last = pe.matmul(bank[MISC][:, t * NE:(t + 1) * NE], xn2T[:, half, t * P:(t + 1) * P], wr_sb[:],
                                     start=True, stop=True)
                last.then_inc(logits_done, 1)
                misc_uses.append((logits_used, half + 1))

            def transpose_weights(half):
                pe.wait_ge(wexp_ready, half + 1)
                misc_free()
                for t in range(HT):
                    last = pe.transpose(bank[MISC][0:NE, t * P:(t + 1) * P], wexp[:, half * HT + t, :], ident[:])
                last.then_inc(wexpT_done, 1)
                misc_uses.append((wexpT_ready, half + 1))

            def output_bias(half):
                misc_free()
                for t in range(HT):
                    last = pe.matmul(bank[MISC][:, t * P:(t + 1) * P], wexpT[:, half, t * P:(t + 1) * P], b2_sb[:],
                                     start=True, stop=True)
                last.then_inc(b2_done, 1)
                misc_uses.append((acc0_ready, half + 1))

            def hidden(n):
                half, e, c = n // HALF_E, n % HALF_E // FC, n % FC
                if c == 0:
                    pe.wait_ge(xe_ready, n // FC + 1)
                    pe.wait_ge(w1part_ready, e + 1)
                if n < len(X_BANK):
                    pe.wait_ge(exp_done, NU * NX_U)
                else:
                    pe.wait_ge(hid_ready, n - len(X_BANK) + 1)
                b, z = bank[X_BANK[n % len(X_BANK)]], (n // FC) % 2
                w = w1_part[:, e, :, c * P:(c + 1) * P]
                pe.matmul(b[:, 0:TOK], w[:, 0, :], xe_part[:, z, 0, :], start=True, stop=False)
                pe.matmul(b[:, 0:TOK], w[:, 0, :], xe_part[:, z, 1, :], start=False, stop=False)
                pe.matmul(b[:, 0:TOK], w[:, 1, :], xe_part[:, z, 0, :], start=False, stop=True).then_inc(f1_done, 1)

            def expert_out(n):
                e, c, m = n % HALF_E // FC, n % FC, n // FC
                if n < FC:
                    pe.wait_ge(s_used, NU * NS_U)
                if c == 0:
                    pe.wait_ge(in_w2[e], 16)
                    if m >= 2:
                        pe.wait_ge(y_used, m - 1)
                pe.wait_ge(hid_ready, n + 1)
                for t in range(HT):
                    last = pe.matmul(bank[S_BANK[m % 2]][:, t * P:(t + 1) * P], hid[:, n % NH_RING, t * P:(t + 1) * P],
                                     w2_sb[:, e, c, :], start=(c == 0 and t == 0), stop=(c == FC - 1 and t == HT - 1),
                                     skip_group_check=True)
                last.then_inc(f2_done, 1)

            def transpose_masks(p):
                pe.wait_ge(ident_ready, 2)
                pe.wait_ge(maskb_ready, NT)
                b = bank[(2, 5)[p]][:].bitcast(BF16)
                if p == 1:
                    pe.wait_ge(va_ready, 1)
                for k in range(2):
                    for t in range(NT):
                        i = 2 * p + k
                        last = pe.transpose(b[:, k * T + t * P:k * T + (t + 1) * P], maskb[:, t, i * P:(i + 1) * P], identb[:])
                last.then_inc(mT_done, 1)

            pe.wait_ge(const_ready, 2)
            pe.wait_ge(xn1T_ready, 1)
            pick(0)
            pick(1)
            pick(2)
            for n in range(G):
                score(n)
            pick(3)
            for n in range(G, NS_U):
                score(n)
                pick(n)
            transpose_masks(0)
            transpose_masks(1)
            pe.wait_ge(in_rows, 16 * 3)
            misc_free()
            pe.transpose(bank[MISC][:, 0:NROWS], rows[:], ident[0:NROWS, 0:NROWS]).then_inc(rows_done, 1)
            misc_uses.append((cols_ready, 1))
            for n in range(NS_U, NS_U + 2):
                score(n)
            transpose_maxima(0)
            for n in range(NS_U + 2, LEAD):
                score(n)
            late = {13: lambda: transpose_output(0), 20: lambda: transpose_output(1), 22: lambda: transpose_normalised(0),
                    24: lambda: project(0), 26: lambda: transpose_output(2), 28: lambda: transpose_xn2(0), 30: lambda: route(0)}
            for n in range(NU * NX_U):
                transposed_scores(n)
                if n + LEAD < NU * NS_U:
                    score(n + LEAD)
                if n % NX_U == 3 and n // NX_U + 1 < NU:
                    transpose_maxima(n // NX_U + 1)
                if n % G == 1 and n >= G + 1:
                    weighted_values(n // G - 1)
                if n in late:
                    late[n]()
            weighted_values(NU * NIP - 1)

            tail = {2: lambda: transpose_output(3), 5: lambda: transpose_weights(0), 7: lambda: output_bias(0),
                    9: lambda: transpose_normalised(1), 11: lambda: project(1), 16: lambda: transpose_xn2(1),
                    18: lambda: route(1), 24: lambda: transpose_weights(1), 26: lambda: output_bias(1)}
            for n in range(NHALF * HALF_E + FC):
                if n < NHALF * HALF_E:
                    hidden(n)
                if n >= FC:
                    expert_out(n - FC)
                if n in tail:
                    tail[n]()

        @block.scalar
        def _(act):
            steps = [0]
            act.dma_start(hn_sb[:], h_neigh.rearrange("(i p) d -> p i d", p=P)).then_inc(in_hn, 16)
            act.wait_ge(early_done, 1)
            act.activation(cols[:, 0:NEARLY], bank[MISC][:, 0:NEARLY], ACT.Copy).then_inc(cols_early_ready, 1)
            act.wait_ge(cols_early_ready, 1)
            act.wait_ge(hT_done, 1)
            act.activation(msgT[:], bank[2][:], ACT.Identity, bias=cols[:, C_E1:C_E1 + 1]).then_inc(msgT_ready, 1)
            act.wait_ge(w_done, 1)
            act.activation(wT[:].rearrange("p a d -> p (a d)"), bank[1][:], ACT.Copy).then_inc(wT_ready, 1)
            act.wait_ge(k_done, 1)
            act.activation(k_full[:], bank[4][:], ACT.Identity, bias=cols[:, C_BK:C_BK + 1]).then_inc(kfull_ready, 1)

            def heads(n):
                what, pair = picks[n]
                act.wait_ge(picked, n + 1)
                for a in range(2):
                    act.activation((KA, QA)[what][0:MAXROW, 2 * pair + a, :],
                                   bank[PICK_BANK[n % len(PICK_BANK)]][64 * a:64 * (a + 1), :], ACT.Copy).then_inc(heads_ready, 1)

            for n in range(H):
                heads(n)
            act.wait_ge(mT_done, 1)
            act.activation(maskT[:, 0:2, :].rearrange("p i t -> p (i t)"), bank[2][:].bitcast(BF16), ACT.Copy).then_inc(maskT_ready, 1)
            act.wait_ge(rows_done, 1)
            act.activation(cols[:, NEARLY:NEARLY + NROWS], bank[MISC][:, 0:NROWS], ACT.Copy).then_inc(cols_ready, 1)
            act.wait_ge(cols_ready, 1)

            def maxima(u):
                act.wait_ge(nmaxT_done, u + 1)
                act.activation(nmaxT[:, u, :], bank[MISC][0:PARTS * G, 0:TOK], ACT.Copy).then_inc(nmaxT_ready, 1)

            def exponential(n):
                act.wait_ge(st_done, n + 1)
                if n >= NP_RING:
                    act.wait_ge(pv_done, n // G - 1)
                act.activation(PT[:, n % NP_RING, :], bank[X_BANK[n % len(X_BANK)]][:], ACT.Exp).then_inc(exp_done, 1)

            def output(u):
                act.wait_ge(pv_done, NIP * (u + 1))
                act.activation(O_sb[:, u, :], bank[O_BANK[u % 2]][:, 0:TOK], ACT.Copy).then_inc(o_ready, 1)

            def w1_rounded(e):
                act.wait_ge(in_w1[e], 16)
                act.activation(w1_part[:, e, 0, :], w1_sb[:, e, :], ACT.Copy).then_inc(w1hi_ready, 1)

            def from_misc(done, dst, ready, half, rows_=P):
                act.wait_ge(done, half + 1)
                act.activation(dst, bank[MISC][0:rows_, 0:TOK], ACT.Copy).then_inc(ready, 1)

            maxima(0)
            for n in range(NU * NX_U):
                exponential(n)
                if n % NX_U == 3 and n // NX_U + 1 < NU:
                    maxima(n // NX_U + 1)
                if n % NX_U == 1 and n > NX_U:
                    output(n // NX_U - 1)
                if n % 2 == 0 and 2 <= n < 2 + 2 * NE:
                    w1_rounded(n // 2 - 1)
                if n == 22:
                    from_misc(onatT_done, o_natT[:, 0, :], onatT_ready, 0)
                if n == 28:
                    from_misc(xn2T_done, xn2T[:, 0, :], xn2T_ready, 0)
            output(NU - 1)
            for n in range(NHALF * HALF_E):
                act.wait_ge(f1_done, n + 1)
                if n >= NH_RING:
                    act.wait_ge(f2_done, n - NH_RING + 1)
                act.activation(hid[:, n % NH_RING, :], bank[X_BANK[n % len(X_BANK)]][:, 0:TOK], ACT.Gelu,
                               bias=cols[:, C_B1 + n % HALF_E:C_B1 + n % HALF_E + 1]).then_inc(hid_ready, 1)
                if n == 5:
                    from_misc(wexpT_done, wexpT[:, 0, :], wexpT_ready, 0, NE)
                if n == 9:
                    from_misc(onatT_done, o_natT[:, 1, :], onatT_ready, 1)
                if n == 16:
                    from_misc(xn2T_done, xn2T[:, 1, :], xn2T_ready, 1)
                if n == 24:
                    from_misc(wexpT_done, wexpT[:, 1, :], wexpT_ready, 1, NE)

        @block.vector
        def _(dve):
            steps = [0]

            def step(ins):
                steps[0] += 1
                ins.then_inc(dve_step, 1)
                dve.wait_ge(dve_step, steps[0])

            dve.memset(pick_q[:].bitcast(F32), 0.0).then_inc(pick_zero, 1)
            dve.memset(pick_k[:].bitcast(F32), 0.0).then_inc(pick_zero, 1)
            dve.wait_ge(pick_zero, 2)
            dve.wait_ge(ident_ready, 1)
            head_rows = ident[:].rearrange("p (h d) -> p h d", d=DH).unsqueeze(2).broadcast_to([P, H, 2, DH])
            for part in range(PARTS):
                q_cols = pick_q[:, part, :, :].rearrange("p h (c r d) -> p h c r d", c=2, d=DH)[:, :, part, :, :]
                k_cols = pick_k[:, part, :, :].rearrange("p h (r c d) -> p h r c d", c=2, d=DH)[:, :, :, part, :]
                dve.tensor_copy(q_cols, head_rows).then_inc(pick_ready, 1)
                dve.tensor_copy(k_cols, head_rows).then_inc(pick_ready, 1)
            dve.wait_ge(in_x, 16)
            for t in range(NT):
                last = dve.bn_stats(stats[:, t, :], x_sb[:, t, :])
            step(last)
            for t in range(NT):
                last = dve.bn_aggr(mv[:, t, :], stats[:, t, :])
            step(last)
            dve.tensor_scalar(var_eps[:], mv[:, :, 1], EPS, None, ALU.add).then_inc(var1_ready, 1)
            dve.wait_ge(rstd1_ready, 1)
            for t in range(NT):
                last = dve.tensor_scalar(xn1[:, t, :], x_sb[:, t, :], mv[:, t, 0:1], rstd[:, t:t + 1], ALU.subtract, ALU.mult)
            last.then_inc(xn1_ready, 1)
            dve.wait_ge(xT_done, 1)
            dve.tensor_copy(xn1T[:], bank[0][:]).then_inc(xn1T_ready, 1)
            dve.wait_ge(kfull_ready, 1)
            step(dve.tensor_copy(k_part[:, 0, :], k_full[:]))
            dve.tensor_tensor(k_part[:, 1, :], k_full[:], k_part[:, 0, :].bitcast(F32), ALU.subtract).then_inc(kpart_ready, 1)

            def additive_mask(t):
                dve.wait_ge(in_adj, 16)
                dve.tensor_scalar(maskb[:, t, :], adj_sb[:, t, :], 0.0, MASKED, ALU.is_equal, ALU.mult).then_inc(maskb_ready, 1)

            additive_mask(0)
            dve.wait_ge(q_done, 1)
            dve.wait_ge(cols_early_ready, 1)
            step(dve.tensor_scalar(q_full[:], bank[3][:], cols[:, C_BQ:C_BQ + 1], float(DH) ** -0.5, ALU.add, ALU.mult))
            step(dve.tensor_copy(q_part[:, 0, :], q_full[:]))
            dve.tensor_tensor(q_part[:, 1, :], q_full[:], q_part[:, 0, :].bitcast(F32), ALU.subtract).then_inc(qpart_ready, 1)
            for t in range(1, NT):
                additive_mask(t)

            def values():
                dve.wait_ge(v_done, 1)
                dve.wait_ge(in_bc, 48)
                dve.wait_ge(const_ready, 4)
                for i in range(NI):
                    last = dve.tensor_tensor(Va[:, i, :, 0:DH], bank[5][:, i * P:(i + 1) * P].rearrange("p (h d) -> p h d", d=DH),
                                             bv_bc[:].rearrange("p (h d) -> p h d", d=DH), ALU.add)
                last.then_inc(va_ready, 1)

            def maximum(n):
                u, r = n // NS_U, n % NS_U
                t, j = tile_of(r)
                if n == 0:
                    dve.wait_ge(maskb_ready, NT)
                dve.wait_ge(s_done, n + 1)
                dve.tensor_tensor_reduce(out=junk[:, n % 2, :], in0=bank[S_BANK[n % 2]][:],
                                         in1=maskb[:, unit[u][0] * HT + t, :], scale=1.0, scalar=-3e38,
                                         op0=ALU.add, op1=ALU.max, accum_out=mx[:, u, t * G + j:t * G + j + 1]).then_inc(s_used, 1)

            def negative_maxima(u):
                dve.wait_ge(s_used, NS_U * (u + 1))
                nm = nmax[:, u, :].rearrange("p (t j) -> p t j", j=G)
                step(dve.tensor_scalar(nmax[:, u, :], mx[:, u, :], LOWEST_MAX, -1.0, ALU.max, ALU.mult))
                step(dve.tensor_copy(nmax_part[:, u, :, 0, :], nm))
                dve.tensor_tensor(nmax_part[:, u, :, 1, :], nm, nmax_part[:, u, :, 0, :].bitcast(F32),
                                  ALU.subtract).then_inc(nmax_ready, 1)

            def normalise(u):
                half, g = unit[u]
                dve.wait_ge(oT_done, u + 1)
                o = bank[MISC][:, 0:TOK].rearrange("p (t j r) -> p t j r", t=HT, j=G)
                d = den[:, u, :].rearrange("p (t j) -> p t j", j=G)
                step(dve.tensor_scalar(d, o[:, :, :, DH], TINY, None, ALU.max))
                step(dve.reciprocal(rden[:, u, :], den[:, u, :]))
                for t in range(HT):
                    r = rden[:, u, t * G:(t + 1) * G].unsqueeze(2).broadcast_to([P, G, DH])
                    last = dve.tensor_tensor(o_nat[:, half, t, G * g:G * g + G, :], o[:, t, :, 0:DH], r, ALU.mult)
                last.then_inc(onat_ready, 1)

            def second_norms(half):
                ts = slice(half * HT, (half + 1) * HT)
                dve.wait_ge(proj_done, half + 1)
                dve.wait_ge(xb_ready, 1)
                dve.tensor_tensor(x2[:, ts, :], bank[MISC][:, 0:TOK].rearrange("p (t d) -> p t d", d=D), xb[:, ts, :],
                                  ALU.add).then_inc(x2_ready, 1)
                dve.wait_ge(x2_ready, half + 1)
                for t in range(half * HT, (half + 1) * HT):
                    last = dve.bn_stats(stats2[:, t, :], x2[:, t, :])
                step(last)
                for t in range(half * HT, (half + 1) * HT):
                    last = dve.bn_aggr(mv2[:, t, :], stats2[:, t, :])
                step(last)
                dve.tensor_scalar(vw[:, ts, 0], mv2[:, ts, 1], EPS, None, ALU.add)
                dve.tensor_scalar(vw[:, ts, 1], mv2[:, ts, 1], 1.0 + EPS, EPS * EPS, ALU.mult, ALU.add).then_inc(vw_ready, 1)

            def second_norms_b(half):
                ts = slice(half * HT, (half + 1) * HT)
                dve.wait_ge(rvw_ready, half + 1)
                for t in range(half * HT, (half + 1) * HT):
                    last = dve.tensor_scalar(xn2[:, t, :], x2[:, t, :], mv2[:, t, 0:1], rvw[:, t, 1:2], ALU.subtract, ALU.mult)
                last.then_inc(xn2_ready, 1)
                step(dve.tensor_tensor(sw[:, ts], vw[:, ts, 1], rvw[:, ts, 1], ALU.mult))
                step(dve.tensor_tensor(sdb[:, ts], sw[:, ts], rvw[:, ts, 0], ALU.mult))

            def router(half):
                ts, tiles = slice(half * HT, (half + 1) * HT), range(half * HT, (half + 1) * HT)
                dve.wait_ge(logits_done, half + 1)
                for t in tiles:
                    k = t - half * HT
                    last = dve.scalar_tensor_tensor(out=logits[:, t, :], in0=bank[MISC][:, k * NE:(k + 1) * NE],
                                                    scalar=sdb[:, t:t + 1], in1=br_bc[:], op0=ALU.mult, op1=ALU.add)
                last.then_inc(logits_used, 1)
                dve.wait_ge(logits_used, half + 1)
                for t in tiles:
                    last = dve.max(top[:, t, :], logits[:, t, :])
                step(last)
                dve.tensor_tensor(gap[:, ts], top[:, ts, 1], top[:, ts, 0], ALU.subtract).then_inc(gap_ready, 1)
                for t in tiles:
                    last = dve.max_index(top_at[:, t, :], top[:, t, :], logits[:, t, :])
                step(last)
                dve.tensor_copy(top_no[:, ts, :], top_at[:, ts, 0:2])

            def router_b(half):
                ts, tiles = slice(half * HT, (half + 1) * HT), range(half * HT, (half + 1) * HT)
                dve.wait_ge(egap_ready, half + 1)
                step(dve.tensor_scalar(dgap[:, ts], egap[:, ts], 1.0, None, ALU.add))
                step(dve.reciprocal(wtop[:, ts, 0], dgap[:, ts]))
                step(dve.tensor_tensor(wtop[:, ts, 1], wtop[:, ts, 0], egap[:, ts], ALU.mult))
                dve.wait_ge(const_ready, 5)
                for t in tiles:
                    dve.tensor_scalar(wfirst[:, t, :], expert_no[:], top_no[:, t, 0:1], wtop[:, t, 0:1], ALU.is_equal, ALU.mult)
                    last = dve.tensor_scalar(wsecond[:, t, :], expert_no[:], top_no[:, t, 1:2], wtop[:, t, 1:2], ALU.is_equal, ALU.mult)
                step(last)
                dve.tensor_tensor(wexp[:, ts, :], wfirst[:, ts, :], wsecond[:, ts, :], ALU.add).then_inc(wexp_ready, 1)

            def start_sum(half):
                ts = slice(half * HT, (half + 1) * HT)
                dve.wait_ge(b2_done, half + 1)
                dve.tensor_tensor(acc[:, 1, ts, :], bank[MISC][:, 0:TOK].rearrange("p (t d) -> p t d", d=D), x2[:, ts, :],
                                  ALU.add).then_inc(acc0_ready, 1)
                dve.wait_ge(acc0_ready, half + 1)

            def expert_in(m):
                half, e = m // NE, m % NE
                if e == 0:
                    dve.wait_ge(cols_ready, 1)
                    dve.wait_ge(xn2T_ready, half + 1)
                if m >= 2:
                    dve.wait_ge(f1_done, FC * (m - 1))
                z = m % 2
                step(dve.tensor_scalar(xe[:, z, :], xn2T[:, half, :], cols[:, C_G + e:C_G + e + 1], cols[:, C_B + e:C_B + e + 1],
                                       ALU.mult, ALU.add))
                step(dve.tensor_copy(xe_part[:, z, 0, :], xe[:, z, :]))
                dve.tensor_tensor(xe_part[:, z, 1, :], xe[:, z, :], xe_part[:, z, 0, :].bitcast(F32), ALU.subtract).then_inc(xe_ready, 1)

            def add_expert(m):
                half, e = m // NE, m % NE
                if e == 0:
                    dve.wait_ge(wexp_ready, half + 1)
                dve.wait_ge(f2_done, FC * (m + 1))
                for k in range(HT):
                    t = half * HT + k
                    last = dve.scalar_tensor_tensor(out=acc[:, e % 2, t, :], in0=bank[S_BANK[m % 2]][:, k * P:(k + 1) * P],
                                                    scalar=wexp[:, t, e:e + 1], in1=acc[:, 1 - e % 2, t, :],
                                                    op0=ALU.mult, op1=ALU.add)
                last.then_inc(y_used, 1)
                dve.wait_ge(y_used, m + 1)

            for n in range(NU * NS_U):
                maximum(n)
                if n % NS_U == NS_U - 1:
                    negative_maxima(n // NS_U)
                if n == 3:
                    values()
                if n == NS_U - 1:
                    dve.wait_ge(mT_done, 2)
                    dve.tensor_copy(maskT[:, 2:4, :].rearrange("p i t -> p (i t)"), bank[5][:].bitcast(BF16)).then_inc(maskT_ready, 1)
                if n == LEAD + 13:
                    normalise(0)
            normalise(1)
            second_norms(0)
            normalise(2)
            second_norms_b(0)
            expert_in(0)
            router(0)
            expert_in(1)
            router_b(0)
            normalise(3)
            start_sum(0)
            for m in range(NHALF * NE):
                if m + 2 < NHALF * NE:
                    expert_in(m + 2)
                add_expert(m)
                if m == 1:
                    second_norms(1)
                if m == 2:
                    second_norms_b(1)
                if m == 3:
                    router(1)
                if m == 4:
                    router_b(1)
                if m == 5:
                    start_sum(1)


_INS = ['x', 'adj', 'L0_gnn_h_neigh', 'L0_gnn_Wq', 'L0_gnn_bq', 'L0_gnn_Wk', 'L0_gnn_bk', 'L0_gnn_Wv', 'L0_gnn_bv',
        'L0_gnn_Wo', 'L0_gnn_bo', 'L0_gnn_E', 'L0_ffn_Wr', 'L0_ffn_br', 'L0_ffn_ln_g', 'L0_ffn_ln_b', 'L0_ffn_W1',
        'L0_ffn_b1', 'L0_ffn_W2', 'L0_ffn_b2']
_OUTS = [((512, 128), 'float32')]


def kernel(**inputs):
    import numpy as _np
    import concourse.bacc as _bacc
    from concourse import mybir as _mybir
    from concourse.bass_utils import run_bass_kernel_spmd as _run

    nc = _bacc.Bacc("TRN2", target_bir_lowering=False, num_devices=1)
    arrays, args = {}, []
    for name in _INS:
        a = _np.ascontiguousarray(inputs[name])
        arrays[f"in_{name}_dram"] = a
        args.append(nc.dram_tensor(f"in_{name}_dram", a.shape, _mybir.dt.from_np(a.dtype), kind="ExternalInput").ap())
    for i, (shape, dtype) in enumerate(_OUTS):
        dt = _mybir.dt.from_np(_np.dtype(dtype))
        args.append(nc.dram_tensor(f"out_{i}_dram", shape, dt, kind="ExternalOutput").ap())
    gnn_ffn_kernel(nc, *args)
    r = _run(nc, [arrays], core_ids=[0])
    got = tuple(r.results[0][f"out_{i}_dram"] for i in range(len(_OUTS)))
    return got[0]
```

```python
from contextlib import ExitStack

import concourse.bass as bass
from concourse import mybir

ALU = mybir.AluOpType
ACT = mybir.ActivationFunctionType
F32 = mybir.dt.float32
F32R = mybir.dt.float32r
BF16 = mybir.dt.bfloat16
I32 = mybir.dt.int32
U32 = mybir.dt.uint32

P = 128
EPS = 1e-5
MASKED = -1e9
LOWEST_MAX = -1e8
TINY = 1e-30
HEAD_ROWS = 32
PARTS = 2


def gnn_ffn_kernel(nc, x, adj, h_neigh, Wq, bq, Wk, bk, Wv, bv, Wo, bo, E, Wr, br, ln_g, ln_b, W1, b1, W2, b2, out):
    T, D = x.shape
    N = h_neigh.shape[0]
    NE, _, F = W1.shape
    NT, NI, FC = T // P, N // P, F // P
    DH = 16
    H = D // DH
    G = 4
    NG = H // G
    HT = 2
    NHALF = NT // HT
    TOK = HT * P
    NU = NHALF * NG
    KROWS = 96
    MAXROW = 4 * DH
    WARM_START, WARM_KEYS = 7, 4
    assert NE == 2 * NU and D == P and N == 512 and T == 512 and H == 8

    NS_U = HT * G
    NIP = NI // 2
    NX_U = NIP * G
    LEAD = NS_U + 6
    NP_RING = 2 * G
    NXE_RING = 3
    NH_RING = 8
    HALF_E = NE * FC
    LAST = NHALF * NE - 1

    C_E1, C_BK, C_BQ, NEARLY = 0, 1, 2, 3
    C_B1, C_G, C_B = NEARLY, NEARLY + NE * FC, NEARLY + NE * FC + NE
    NROWS = NE * FC + 2 * NE

    with ExitStack() as ctx:
        def sb(name, shape, dt):
            return ctx.enter_context(nc.sbuf_tensor(name, shape, dt))

        def sem(name):
            return ctx.enter_context(nc.semaphore(name))

        bank = [ctx.enter_context(nc.psum_tensor(f"bank{i}", [P, 512], F32)) for i in range(8)]
        S_BANK, X_BANK, O_BANK, MISC = [0, 1], [2, 3, 4], [5, 6], 7
        LAST_BANK = [S_BANK[LAST % 2], O_BANK[0]]

        x_sb = sb("x_sb", [P, NT, D], F32)
        adj_sb = sb("adj_sb", [P, NT, N], I32)
        hn_sb = sb("hn_sb", [P, NI, D], F32)
        w_sb = sb("w_sb", [P, 3, D], F32)
        wo_sb = sb("wo_sb", [P, D], F32)
        row_e1 = sb("row_e1", [1, D], F32)
        rows_qk = sb("rows_qk", [2, D], F32)
        rows = sb("rows", [NROWS, D], F32)
        bv_row = sb("bv_row", [1, D], F32)
        ones_row = sb("ones_row", [1, P], F32)
        bo_bc = sb("bo_bc", [P, D], F32)
        br_bc = sb("br_bc", [P, NE], F32)
        wr_sb = sb("wr_sb", [P, NE], F32)
        b2_sb = sb("b2_sb", [NE, D], F32)
        w1_sb = sb("w1_sb", [P, NE, F], F32)
        w2_sb = sb("w2_sb", [P, NE, FC, D], F32)
        ident = sb("ident", [P, P], F32)
        identb = sb("identb", [P, P], BF16)
        pick_q = sb("pick_q", [P, PARTS, H, MAXROW], F32R)
        pick_k = sb("pick_k", [P, PARTS, H, MAXROW], F32R)
        warm = sb("warm", [P, 512], BF16)
        scrap = sb("scrap", [P, 1], F32)
        half_pow = sb("half_pow", [P, NT], F32)
        euler = sb("euler", [P, HT], F32)
        expert_no = sb("expert_no", [P, NE], F32)
        stats = sb("stats", [P, NT, 6], F32)
        mv = sb("mv", [P, NT, 2], F32)
        var_eps = sb("var_eps", [P, NT], F32)
        rstd = sb("rstd", [P, NT], F32)
        xn1 = sb("xn1", [P, NT, D], F32)
        xb = sb("xb", [P, NT, D], F32)
        xn1T = sb("xn1T", [P, T], F32)
        wT = sb("wT", [P, 4, D], F32)
        cols = sb("cols", [P, NEARLY + NROWS], F32)
        msgT = sb("msgT", [P, N], F32)
        q_part = sb("q_part", [P, PARTS, T], F32R)
        k_part = sb("k_part", [P, PARTS, N], F32R)
        QA = sb("QA", [KROWS, H, T], F32R)
        KA = sb("KA", [KROWS, H, N], F32R)
        Va = sb("Va", [P, NI, H, HEAD_ROWS], F32)
        maskb = sb("maskb", [P, NT, N], BF16)
        maskT = sb("maskT", [P, NI, T], BF16)
        junk = sb("junk", [P, 2, N], BF16)
        mx = sb("mx", [P, NU, NS_U], F32)
        nmax = sb("nmax", [P, NU, NS_U], F32)
        nmax_part = sb("nmax_part", [P, NU + 1, HT, PARTS * G], F32R)
        nmaxT = sb("nmaxT", [PARTS * G, NU + 1, TOK], F32)
        PT = sb("PT", [P, NP_RING, 512], F32)
        O_sb = sb("O_sb", [P, NU, TOK], F32)
        den = sb("den", [P, NU, HT * G], F32)
        rden = sb("rden", [P, NU, HT * G], F32)
        o_nat = sb("o_nat", [P, NHALF, HT, H, DH], F32)
        o_natT = sb("o_natT", [P, NHALF, TOK], F32)
        x2 = sb("x2", [P, NT, D], F32)
        stats2 = sb("stats2", [P, NT, 6], F32)
        mv2 = sb("mv2", [P, NT, 2], F32)
        vw = sb("vw", [P, NT, 2], F32)
        rvw = sb("rvw", [P, NT, 2], F32)
        sw = sb("sw", [P, NT], F32)
        sdb = sb("sdb", [P, NT], F32)
        xn2 = sb("xn2", [P, NT, D], F32)
        xn2T = sb("xn2T", [P, NHALF, TOK], F32)
        logits = sb("logits", [P, NT, NE], F32)
        top = sb("top", [P, NT, 8], F32)
        top_at = sb("top_at", [P, NT, 8], U32)
        top_no = sb("top_no", [P, NT, 2], F32)
        gap = sb("gap", [P, NT], F32)
        egap = sb("egap", [P, NT], F32)
        dgap = sb("dgap", [P, NT], F32)
        wtop = sb("wtop", [P, NT, 2], F32)
        wfirst = sb("wfirst", [P, NT, NE], F32)
        wsecond = sb("wsecond", [P, NT, NE], F32)
        wexp = sb("wexp", [P, NT, NE], F32)
        wexpT = sb("wexpT", [NE, NHALF, TOK], F32)
        w1_part = sb("w1_part", [P, NE, PARTS, F], F32R)
        xe = sb("xe", [P, NXE_RING, TOK], F32)
        xe_part = sb("xe_part", [P, NXE_RING, PARTS, TOK], F32R)
        hid = PT[:, :, 0:TOK]
        acc = sb("acc", [P, 2, NT, D], F32)

        in_hn, in_wo, in_rows, in_bv, in_adj = (sem(n) for n in ("in_hn", "in_wo", "in_rows", "in_bv", "in_adj"))
        in_x = [sem(f"in_x_{half}") for half in range(NHALF)]
        in_e1, in_bias_rows, in_wk, in_wq, in_wv = (sem(n) for n in ("in_e1", "in_bias_rows", "in_wk", "in_wq", "in_wv"))
        e1_ready, cols_early_ready, early_done = sem("e1_ready"), sem("cols_early_ready"), sem("early_done")
        wq_done, wk_done, wv_done, wqT_ready, wkT_ready, wvT_ready, khi_ready = (
            sem(n) for n in ("wq_done", "wk_done", "wv_done", "wqT_ready", "wkT_ready", "wvT_ready", "khi_ready"))
        qhi_ready, va_const_ready, expert_no_ready, warm_ready = (
            sem(n) for n in ("qhi_ready", "va_const_ready", "expert_no_ready", "warm_ready"))
        in_adj_late, in_bias_bc = sem("in_adj_late"), sem("in_bias_bc")
        in_router, in_w1, in_w2 = sem("in_router"), [sem(f"in_w1_{e}") for e in range(NE)], [sem(f"in_w2_{e}") for e in range(NE)]
        ident_ready, pick_zero, pick_ready, const_ready, pool_step = sem("ident_ready"), sem("pick_zero"), sem("pick_ready"), sem("const_ready"), sem("pool_step")
        dve_step = sem("dve_step")
        var1_ready, rstd1_ready, xn1_ready, xn1T_ready = sem("var1_ready"), sem("rstd1_ready"), sem("xn1_ready"), sem("xn1T_ready")
        xT_done, hT_done, rows_done, q_done, k_done, v_done, mT_done = (
            sem(n) for n in ("xT_done", "hT_done", "rows_done", "q_done", "k_done", "v_done", "mT_done"))
        cols_ready, msgT_ready, qpart_ready, kpart_ready = (
            sem(n) for n in ("cols_ready", "msgT_ready", "qpart_ready", "kpart_ready"))
        va_ready, maskb_ready, maskT_ready, woT_ready, xb_ready = (
            sem(n) for n in ("va_ready", "maskb_ready", "maskT_ready", "woT_ready", "xb_ready"))
        maskb_late_ready = sem("maskb_late_ready")
        picked, heads_ready = sem("picked"), sem("heads_ready")
        s_done, s_used = sem("s_done"), sem("s_used")
        nmax_ready, nmaxT_done, nmaxT_ready, nmax_in = sem("nmax_ready"), sem("nmaxT_done"), sem("nmaxT_ready"), sem("nmax_in")
        nmax_in_first = sem("nmax_in_first")
        st_done, exp_done, pv_done, o_ready = sem("st_done"), sem("exp_done"), sem("pv_done"), sem("o_ready")
        oT_done, onat_ready, onatT_done, onatT_ready, proj_done, x2_ready = (
            sem(n) for n in ("oT_done", "onat_ready", "onatT_done", "onatT_ready", "proj_done", "x2_ready"))
        vw_ready, rvw_ready, xn2_ready, xn2T_done, xn2T_ready = (
            sem(n) for n in ("vw_ready", "rvw_ready", "xn2_ready", "xn2T_done", "xn2T_ready"))
        logits_done, gap_ready, egap_ready, wexp_ready, wexpT_done, wexpT_ready, b2_done, acc0_ready, logits_used = (
            sem(n) for n in ("logits_done", "gap_ready", "egap_ready", "wexp_ready", "wexpT_done", "wexpT_ready", "b2_done", "acc0_ready", "logits_used"))
        last_done, last_added = sem("last_done"), sem("last_added")
        w1hi_ready, w1part_ready, xe_ready, f1_done, hid_ready, f2_done, y_used, stored = (
            sem(n) for n in ("w1hi_ready", "w1part_ready", "xe_ready", "f1_done", "hid_ready", "f2_done", "y_used", "stored"))

        block = ctx.enter_context(nc.Block())

        maxima_of = [(0, 0, G // 2), (0, G // 2, G)] + [(u, 0, G) for u in range(1, NU)]
        unit = [(half, g) for half in range(NHALF) for g in range(NG)]
        picks = [(what, pair) for pair in range(H // 2) for what in (0, 1)]
        picks += [(2, pair) for pair in range(H // 2)]
        PICK_BANK = [5] + [(4, 6, 3)[n % 3] for n in range(1, H)] + [6] * (H // 2)
        pick_at = {2: H, 4: H + 1, 6: H + 2, 8: H + 3}

        MAXIMA_BANK = [MISC] * NU + [S_BANK[0]]

        def tile_of(r):
            return r // 2 % HT, 2 * (r // (2 * HT)) + r % 2

        @block.sync
        def _(sp):
            sp.dma_start(x_sb[:, 0:HT, :], x[0:TOK, :].rearrange("(t p) d -> p t d", p=P)).then_inc(in_x[0], 16)
            sp.dma_start(w_sb[:, 1, :], Wk).then_inc(in_wk, 16)
            sp.dma_start(rows_qk[0:1, :], bk.rearrange("(a d) -> a d", a=1)).then_inc(in_bias_rows, 16)
            sp.dma_start(rows_qk[1:2, :], bq.rearrange("(a d) -> a d", a=1)).then_inc(in_bias_rows, 16)
            sp.dma_start(adj_sb[:, 0:HT, :], adj[0:TOK, :].rearrange("(t p) n -> p t n", p=P)).then_inc(in_adj, 16)
            sp.dma_start(w_sb[:, 2, :], Wv).then_inc(in_wv, 16)
            sp.dma_start(adj_sb[:, HT:NT, :], adj[TOK:T, :].rearrange("(t p) n -> p t n", p=P)).then_inc(in_adj_late, 16)
            sp.dma_start(bv_row[:], bv.rearrange("(a d) -> a d", a=1)).then_inc(in_bv, 16)
            sp.dma_start(wo_sb[:], Wo).then_inc(in_wo, 16)
            sp.dma_start(rows[0:NE * FC, :], b1.rearrange("e (c p) -> (e c) p", p=P)).then_inc(in_rows, 16)
            sp.dma_start(rows[NE * FC:NE * FC + NE, :], ln_g).then_inc(in_rows, 16)
            sp.dma_start(rows[NE * FC + NE:NROWS, :], ln_b).then_inc(in_rows, 16)
            for e in range(NE):
                sp.dma_start(w1_sb[:, e, :], W1[e]).then_inc(in_w1[e], 16)
            for m, (u, a, b) in enumerate(maxima_of):
                half, g = unit[u]
                sp.wait_ge(nmaxT_ready, m + 1)
                sp.dma_start(QA[MAXROW:MAXROW + PARTS, G * g + a:G * g + b, half * TOK:(half + 1) * TOK].bitcast(F32),
                             nmaxT[0:PARTS * (b - a), m, :]).then_inc(nmax_in if m else nmax_in_first, 16)
                if b == G:
                    for e in (2 * u, 2 * u + 1):
                        sp.dma_start(w2_sb[:, e, :, :], W2[e].rearrange("(c p) d -> p c d", p=P)).then_inc(in_w2[e], 16)
            sp.wait_ge(y_used, NE)
            sp.dma_start(out[0:TOK, :].rearrange("(t p) d -> p t d", p=P), acc[:, (NE - 1) % 2, 0:HT, :]).then_inc(stored, 16)
            for t in range(HT, NT):
                if t < NT - 1:
                    sp.wait_ge(last_added, t - HT + 1)
                else:
                    sp.wait_ge(y_used, LAST + 1)
                sp.dma_start(out[t * P:(t + 1) * P, :], acc[:, (NE - 1) % 2, t, :]).then_inc(stored, 16)
            sp.wait_ge(stored, 16 * (1 + HT))

        @block.gpsimd
        def _(pool):
            steps = [0]

            def step(ins):
                steps[0] += 1
                ins.then_inc(pool_step, 1)
                pool.wait_ge(pool_step, steps[0])

            pool.dma_start(row_e1[:], E[1:2, :]).then_inc(in_e1, 16)
            step(pool.memset(ident[:], 0.0))
            pool.affine_select(out=ident[:], in_=ident[:], compare_op=ALU.not_equal, fill=1.0, base=0,
                               pattern=[[-1, P]], channel_multiplier=1).then_inc(ident_ready, 1)
            pool.memset(half_pow[:], -0.5)
            step(pool.memset(euler[:], 2.718281828459045))

            def rest_rows(dst, value):
                rest[0] += 1
                pool.memset(dst.bitcast(F32), value).then_inc(const_ready, 1)

            def first_rstd(half):
                pool.wait_ge(const_ready, rest[0])
                pool.wait_ge(var1_ready, half + 1)
                pool.tensor_tensor(rstd[:, half * HT:(half + 1) * HT], var_eps[:, half * HT:(half + 1) * HT],
                                   half_pow[:, 0:HT], ALU.pow).then_inc(rstd1_ready, 1)
                pool.wait_ge(rstd1_ready, half + 1)

            rest = [0]
            rest_rows(QA[MAXROW:KROWS, 0:G, 0:TOK], 0.0)
            first_rstd(0)
            rest_rows(KA[MAXROW:KROWS, 0:G, :], 1.0)
            first_rstd(1)
            step(pool.memset(identb[:], 0.0))
            pool.affine_select(out=identb[:], in_=identb[:], compare_op=ALU.not_equal, fill=1.0, base=0,
                               pattern=[[-1, P]], channel_multiplier=1).then_inc(ident_ready, 1)
            pool.wait_ge(ident_ready, 2)
            rest_rows(QA[MAXROW:KROWS, G:H, 0:TOK], 0.0)
            rest_rows(KA[MAXROW:KROWS, G:H, :], 1.0)
            pool.wait_ge(const_ready, rest[0])
            step(pool.memset(Va[:], 0.0))
            pool.memset(Va[:, :, :, DH:DH + 1], 1.0).then_inc(va_const_ready, 1)
            pool.wait_ge(va_const_ready, 1)
            rest_rows(QA[MAXROW:KROWS, :, TOK:T], 0.0)
            pool.wait_ge(const_ready, rest[0])
            pool.wait_ge(in_adj_late, 16)
            for t in range(HT, NT):
                pool.tensor_scalar(maskb[:, t, :], adj_sb[:, t, :], 0.0, MASKED, ALU.is_equal, ALU.mult).then_inc(maskb_late_ready, 1)
            pool.iota(expert_no[:], pattern=[[1, NE]], base=0, channel_multiplier=0,
                      allow_small_or_imprecise_dtypes=True).then_inc(expert_no_ready, 1)
            pool.dma_start(bo_bc[:], bo.partition_broadcast(P)).then_inc(in_bias_bc, 16)
            pool.dma_start(br_bc[:], br.partition_broadcast(P)).then_inc(in_bias_bc, 16)
            pool.dma_start(wr_sb[:], Wr).then_inc(in_router, 16)
            pool.dma_start(b2_sb[:], b2).then_inc(in_router, 16)
            pool.wait_ge(in_bias_bc, 32)
            for t in range(NT):
                last = pool.tensor_tensor(xb[:, t, :], x_sb[:, t, :], bo_bc[:], ALU.add)
            last.then_inc(xb_ready, 1)
            def w1_rest(e):
                pool.wait_ge(w1hi_ready, e + 1)
                pool.tensor_tensor(w1_part[:, e, 1, :], w1_sb[:, e, :], w1_part[:, e, 0, :].bitcast(F32),
                                   ALU.subtract).then_inc(w1part_ready, 1)

            for e in range(NE // 2):
                w1_rest(e)
            for half in range(NHALF):
                ts = slice(half * HT, (half + 1) * HT)
                pool.wait_ge(vw_ready, half + 1)
                for k in (1, 0):
                    pool.tensor_tensor(rvw[:, ts, k], vw[:, ts, k], half_pow[:, 0:HT], ALU.pow).then_inc(rvw_ready, 1)
                pool.wait_ge(gap_ready, half + 1)
                pool.tensor_tensor(egap[:, ts], euler[:], gap[:, ts], ALU.pow).then_inc(egap_ready, 1)
                if half == 0:
                    for e in range(NE // 2, NE):
                        w1_rest(e)

        @block.tensor
        def _(pe):
            misc_uses = [(cols_early_ready, 2)]

            def keep_warm(times):
                for _ in range(times):
                    pe.matmul(bank[2][:], warm[:, 0:P], warm[:], start=True, stop=True)

            pe.wait_ge(warm_ready, 1)
            keep_warm(WARM_START)
            pe.wait_ge(ident_ready, 1)
            pe.wait_ge(in_e1, 16)
            pe.transpose(bank[MISC][:, C_E1:C_E1 + 1], row_e1[:], ident[0:1, 0:1]).then_inc(early_done, 1)
            pe.wait_ge(in_hn, 16)
            for i in range(NI):
                last = pe.transpose(bank[2][:, i * P:(i + 1) * P], hn_sb[:, i, :], ident[:])
            last.then_inc(hT_done, 1)
            pe.wait_ge(in_wk, 16)
            pe.transpose(bank[1][:, P:2 * P], w_sb[:, 1, :], ident[:]).then_inc(wk_done, 1)
            pe.wait_ge(in_wq, 16)
            pe.transpose(bank[6][:, 0:P], w_sb[:, 0, :], ident[:]).then_inc(wq_done, 1)

            def transpose_xn1(half):
                pe.wait_ge(xn1_ready, half + 1)
                if half == 1:
                    misc_free()
                for k in range(HT):
                    last = pe.transpose(bank[(0, MISC)[half]][:, k * P:(k + 1) * P], xn1[:, half * HT + k, :], ident[:])
                last.then_inc(xT_done, 1)
                if half == 1:
                    misc_uses.append((xn1T_ready, 2))

            def project_q(half):
                pe.wait_ge(xn1T_ready, half + 1)
                pe.wait_ge(wqT_ready, 1)
                b = bank[(3, 6)[half]][:, half * TOK:(half + 1) * TOK]
                pe.matmul(b, wT[:, 0, :], xn1T[:, half * TOK:(half + 1) * TOK], start=True, stop=True).then_inc(q_done, 1)

            def transpose_wv():
                pe.wait_ge(in_wv, 16)
                pe.wait_ge(wqT_ready, 1)
                pe.transpose(bank[6][:, 0:P], w_sb[:, 2, :], ident[:]).then_inc(wv_done, 1)

            def project_v(tiles):
                pe.wait_ge(wvT_ready, 1)
                pe.wait_ge(in_bv, 16)
                for i in tiles:
                    pe.matmul(bank[5][:, i * P:(i + 1) * P], msgT[:, i * P:(i + 1) * P], wT[:, 2, :], start=True, stop=False)
                    last = pe.matmul(bank[5][:, i * P:(i + 1) * P], ones_row[:], bv_row[:], start=False, stop=True)
                last.then_inc(v_done, 1)

            transpose_xn1(0)
            pe.wait_ge(in_bias_rows, 32)
            pe.wait_ge(e1_ready, 1)
            pe.transpose(bank[MISC][:, C_BK:C_BQ + 1], rows_qk[:], ident[0:2, 0:2]).then_inc(early_done, 1)
            pe.wait_ge(wkT_ready, 1)
            pe.wait_ge(msgT_ready, 1)
            pe.matmul(bank[4][:], wT[:, 1, :], msgT[:], start=True, stop=True).then_inc(k_done, 1)
            project_q(0)
            transpose_wv()
            keep_warm(WARM_KEYS)

            def pick(n):
                what, pair = picks[n]
                half = max(what - 1, 0)
                at = slice(0, N) if what == 0 else slice(half * TOK, (half + 1) * TOK)
                src, pick_w = (k_part, pick_k) if what == 0 else (q_part, pick_q)
                if what or n == PICK_BANK.index(3):
                    pe.wait_ge(qpart_ready, half + 1)
                pe.wait_ge(pick_ready, 2 * PARTS)
                if n == PICK_BANK.index(6):
                    pe.wait_ge(wvT_ready, 1)
                former = [m for m in range(n) if PICK_BANK[m] == PICK_BANK[n]]
                if former:
                    pe.wait_ge(heads_ready, evacuated(former[-1], 1))
                b = bank[PICK_BANK[n]]
                for part in range(PARTS):
                    if what == 0:
                        pe.wait_ge((khi_ready, kpart_ready)[part], 1)
                    last = pe.matmul(b[:, at], pick_w[:, part, 2 * pair:2 * pair + 2, :].rearrange("p a r -> p (a r)"),
                                     src[:, part, at], start=(part == 0), stop=(part == PARTS - 1))
                last.then_inc(picked, 1)

            def evacuated(n, a):
                return 2 * (n - n % 2) + 2 * a + n % 2 + 1 if n < H else 2 * n + a + 1

            def score(n):
                u, r = n // NS_U, n % NS_U
                half, g = unit[u]
                t, j = tile_of(r)
                t += half * HT
                if n == NS_U:
                    pe.wait_ge(const_ready, 4)
                if n == NG * NS_U:
                    pe.wait_ge(const_ready, 5)
                if t % HT == 0:
                    pair = (G * g + j) // 2
                    last_pick = max(picks.index((1 + half, pair)), picks.index((0, pair)))
                    pe.wait_ge(heads_ready, evacuated(last_pick, j % 2))
                if n >= 2:
                    pe.wait_ge(s_used, n - 1)
                pe.matmul(bank[S_BANK[n % 2]][:], QA[:, G * g + j, t * P:(t + 1) * P], KA[:, G * g + j, :],
                          start=True, stop=True).then_inc(s_done, 1)

            def transpose_maxima(m):
                rows_m = PARTS * (maxima_of[m][2] - maxima_of[m][1])
                pe.wait_ge(nmax_ready, m + 1)
                if m < NU:
                    misc_free()
                for t in range(HT):
                    last = pe.transpose(bank[MAXIMA_BANK[m]][0:rows_m, t * P:(t + 1) * P],
                                        nmax_part[:, m, t, 0:rows_m].bitcast(F32), ident[:])
                last.then_inc(nmaxT_done, 1)
                if m < NU:
                    misc_uses.append((nmaxT_ready, m + 1))

            def misc_free():
                if misc_uses:
                    pe.wait_ge(*misc_uses[-1])

            def transposed_scores(n):
                u, r = n // NX_U, n % NX_U
                half, g = unit[u]
                ip, head = r // G, G * g + r % G
                if n == 0:
                    pe.wait_ge(nmax_in_first, 16)
                elif r == 0:
                    pe.wait_ge(nmax_in, 16 * (u + 1))
                if n == G // 2:
                    pe.wait_ge(nmax_in, 16)
                if n == 0:
                    pe.wait_ge(heads_ready, 2 * H)
                if n % (NG * NX_U) == 0:
                    pe.wait_ge(maskT_ready, half + 1)
                if n >= len(X_BANK):
                    pe.wait_ge(exp_done, n - len(X_BANK) + 1)
                b = bank[X_BANK[n % len(X_BANK)]]
                pe.matmul(b[:], identb[:], maskT[:, 2 * ip:2 * ip + 2, half * TOK:(half + 1) * TOK], start=True, stop=False)
                for k in range(2):
                    i = 2 * ip + k
                    last = pe.matmul(b[:, k * TOK:(k + 1) * TOK], KA[:, head, i * P:(i + 1) * P],
                                     QA[:, head, half * TOK:(half + 1) * TOK], start=False, stop=(k == 1))
                last.then_inc(st_done, 1)

            def weighted_values(q):
                u, ip = q // NIP, q % NIP
                half, g = unit[u]
                if q == 0:
                    pe.wait_ge(va_ready, 1)
                if ip == 0 and u >= 2:
                    pe.wait_ge(o_ready, u - 1)
                pe.wait_ge(exp_done, G * (q + 1))
                for k in range(2):
                    i = 2 * ip + k
                    for j in range(G):
                        last = pe.matmul(bank[O_BANK[u % 2]][HEAD_ROWS * j:HEAD_ROWS * (j + 1), 0:TOK],
                                         Va[:, i, G * g + j, :], PT[:, (G * q + j) % NP_RING, k * TOK:(k + 1) * TOK],
                                         start=(i == 0), stop=(i == NI - 1), skip_group_check=True)
                last.then_inc(pv_done, 1)

            def transpose_output(u):
                pe.wait_ge(o_ready, u + 1)
                misc_free()
                for t in range(HT):
                    last = pe.transpose(bank[MISC][:, t * P:(t + 1) * P], O_sb[:, u, t * P:(t + 1) * P], ident[:])
                last.then_inc(oT_done, 1)
                misc_uses.append((onat_ready, u + 1))

            def transpose_normalised(half):
                misc_free()
                for t in range(HT):
                    last = pe.transpose(bank[MISC][:, t * P:(t + 1) * P],
                                        o_nat[:, half, t, :, :].rearrange("p h d -> p (h d)"), ident[:])
                last.then_inc(onatT_done, 1)
                misc_uses.append((onatT_ready, half + 1))

            def project(half):
                misc_free()
                for t in range(HT):
                    last = pe.matmul(bank[MISC][:, t * P:(t + 1) * P], o_natT[:, half, t * P:(t + 1) * P], wT[:, 3, :],
                                     start=True, stop=True)
                last.then_inc(proj_done, 1)
                misc_uses.append((x2_ready, half + 1))

            def transpose_xn2(half):
                pe.wait_ge(xn2_ready, half + 1)
                misc_free()
                for t in range(HT):
                    last = pe.transpose(bank[MISC][:, t * P:(t + 1) * P], xn2[:, half * HT + t, :], ident[:])
                last.then_inc(xn2T_done, 1)
                misc_uses.append((xn2T_ready, half + 1))

            def route(half):
                pe.wait_ge(in_router, 32)
                misc_free()
                for t in range(HT):
                    last = pe.matmul(bank[MISC][:, t * NE:(t + 1) * NE], xn2T[:, half, t * P:(t + 1) * P], wr_sb[:],
                                     start=True, stop=True)
                last.then_inc(logits_done, 1)
                misc_uses.append((logits_used, half + 1))

            def transpose_weights(half):
                pe.wait_ge(wexp_ready, half + 1)
                misc_free()
                for t in range(HT):
                    last = pe.transpose(bank[MISC][0:NE, t * P:(t + 1) * P], wexp[:, half * HT + t, :], ident[:])
                last.then_inc(wexpT_done, 1)
                misc_uses.append((wexpT_ready, half + 1))

            def output_bias(half):
                misc_free()
                for t in range(HT):
                    last = pe.matmul(bank[MISC][:, t * P:(t + 1) * P], wexpT[:, half, t * P:(t + 1) * P], b2_sb[:],
                                     start=True, stop=True)
                last.then_inc(b2_done, 1)
                misc_uses.append((acc0_ready, half + 1))

            def hidden(n):
                half, e, c = n // HALF_E, n % HALF_E // FC, n % FC
                if c == 0:
                    pe.wait_ge(xe_ready, n // FC + 1)
                    pe.wait_ge(w1part_ready, e + 1)
                if n < len(X_BANK):
                    pe.wait_ge(exp_done, NU * NX_U - len(X_BANK) + n + 1)
                else:
                    pe.wait_ge(hid_ready, n - len(X_BANK) + 1)
                b, z = bank[X_BANK[(NU * NX_U + n) % len(X_BANK)]], (n // FC) % NXE_RING
                w = w1_part[:, e, :, c * P:(c + 1) * P]
                pe.matmul(b[:, 0:TOK], w[:, 0, :], xe_part[:, z, 0, :], start=True, stop=False)
                pe.matmul(b[:, 0:TOK], w[:, 0, :], xe_part[:, z, 1, :], start=False, stop=False)
                pe.matmul(b[:, 0:TOK], w[:, 1, :], xe_part[:, z, 0, :], start=False, stop=True).then_inc(f1_done, 1)

            def expert_out(n):
                e, c, m = n % HALF_E // FC, n % FC, n // FC
                if n < FC:
                    pe.wait_ge(s_used, NU * NS_U)
                if c == 0:
                    pe.wait_ge(in_w2[e], 16)
                    if m >= 2:
                        pe.wait_ge(y_used, m - 1)
                pe.wait_ge(hid_ready, n + 1)
                for t in range(HT):
                    last = pe.matmul(bank[S_BANK[m % 2]][:, t * P:(t + 1) * P], hid[:, n % NH_RING, t * P:(t + 1) * P],
                                     w2_sb[:, e, c, :], start=(c == 0 and t == 0), stop=(c == FC - 1 and t == HT - 1),
                                     skip_group_check=True)
                last.then_inc(f2_done, 1)

            def transpose_masks(half):
                pe.wait_ge(ident_ready, 2)
                if half == 0:
                    pe.wait_ge(maskb_ready, HT)
                else:
                    pe.wait_ge(maskb_late_ready, HT)
                    misc_free()
                b = bank[(2, MISC)[half]][:].bitcast(BF16)
                for i in range(NI):
                    for k in range(HT):
                        last = pe.transpose(b[:, i * TOK + k * P:i * TOK + (k + 1) * P],
                                            maskb[:, half * HT + k, i * P:(i + 1) * P], identb[:])
                last.then_inc(mT_done, 1)
                if half == 1:
                    misc_uses.append((maskT_ready, 2))

            pick(0)
            pick(1)
            transpose_masks(0)
            pe.wait_ge(const_ready, 2)
            for n in range(NS_U):
                score(n)
                if n == 5:
                    transpose_maxima(0)
                if n < H - 2:
                    pick(n + 2)
                if n == 6:
                    transpose_xn1(1)
                if n == 7:
                    pe.wait_ge(heads_ready, evacuated(0, 1))
                    project_v(range(NI // 2))
            for n in range(NS_U, NS_U + 2):
                score(n)
            transpose_maxima(1)
            score(NS_U + 2)
            scored = NS_U + 3

            def transpose_rows():
                pe.wait_ge(in_rows, 16 * 3)
                pe.wait_ge(in_wo, 16)
                misc_free()
                pe.transpose(bank[MISC][:, 0:NROWS], rows[:], ident[0:NROWS, 0:NROWS])
                pe.transpose(bank[MISC][:, P:2 * P], wo_sb[:], ident[:]).then_inc(rows_done, 1)
                misc_uses.append((woT_ready, 1))

            for n in range(NU * NX_U):
                transposed_scores(n)
                if n == 0:
                    project_q(1)
                if n == 1:
                    project_v(range(NI // 2, NI))
                if n in pick_at:
                    pick(pick_at[n])
                while scored < min(n + 1 + LEAD, 2 * n + 2 + NS_U + 3, NU * NS_U):
                    score(scored)
                    scored += 1
                if n % NX_U == 3 and n // NX_U + 1 < NU:
                    transpose_maxima(n // NX_U + 2)
                if n == 5:
                    transpose_masks(1)
                if n == 7:
                    transpose_rows()
                if n == 13:
                    transpose_output(0)
                if n == 19:
                    transpose_output(1)
                if n == 21:
                    transpose_normalised(0)
                if n == 22:
                    project(0)
                if n == 26:
                    transpose_xn2(0)
                if n == 28:
                    route(0)
                if n % G == 1 and n >= G + 1:
                    weighted_values(n // G - 1)

            for n in range(NHALF * HALF_E):
                hidden(n)
                if n >= FC:
                    expert_out(n - FC)
                if n == 1:
                    weighted_values(NU * NIP - 1)
                if n == 2:
                    transpose_output(2)
                if n == 5:
                    transpose_output(3)
                if n == 7:
                    transpose_weights(0)
                if n == 9:
                    output_bias(0)
                if n == 12:
                    transpose_normalised(1)
                if n == 14:
                    project(1)
                if n == 20:
                    transpose_xn2(1)
                if n == 22:
                    route(1)
                if n == 27:
                    transpose_weights(1)
                if n == 29:
                    output_bias(1)

            pe.wait_ge(y_used, LAST - 1)
            for t in range(HT):
                for c in range(FC):
                    n = NHALF * HALF_E - FC + c
                    pe.wait_ge(hid_ready, n + 1)
                    last = pe.matmul(bank[LAST_BANK[t]][:, 0:P], hid[:, n % NH_RING, t * P:(t + 1) * P],
                                     w2_sb[:, NE - 1, c, :], start=(c == 0), stop=(c == FC - 1))
                last.then_inc(last_done, 1)

        @block.scalar
        def _(act):
            act.dma_start(hn_sb[:], h_neigh.rearrange("(i p) d -> p i d", p=P)).then_inc(in_hn, 16)
            act.dma_start(w_sb[:, 0, :], Wq).then_inc(in_wq, 16)
            act.dma_start(x_sb[:, HT:NT, :], x[TOK:T, :].rearrange("(t p) d -> p t d", p=P)).then_inc(in_x[1], 16)
            act.wait_ge(warm_ready, 1)
            act.activation(scrap[:], warm[:, 0:1], ACT.Exp)
            act.wait_ge(early_done, 1)
            act.activation(cols[:, C_E1:C_E1 + 1], bank[MISC][:, C_E1:C_E1 + 1], ACT.Copy).then_inc(e1_ready, 1)
            act.wait_ge(e1_ready, 1)
            act.wait_ge(hT_done, 1)
            act.activation(msgT[:], bank[2][:], ACT.Identity, bias=cols[:, C_E1:C_E1 + 1]).then_inc(msgT_ready, 1)
            act.wait_ge(early_done, 2)
            act.activation(cols[:, C_BK:C_BK + 1], bank[MISC][:, C_BK:C_BK + 1], ACT.Copy).then_inc(cols_early_ready, 1)
            act.activation(cols[:, C_BQ:C_BQ + 1], bank[MISC][:, C_BQ:C_BQ + 1], ACT.Copy, scale=float(DH) ** -0.5).then_inc(cols_early_ready, 1)
            act.wait_ge(cols_early_ready, 2)
            act.wait_ge(k_done, 1)
            act.activation(k_part[:, 0, :], bank[4][:], ACT.Identity, bias=cols[:, C_BK:C_BK + 1]).then_inc(khi_ready, 1)
            act.wait_ge(q_done, 1)
            act.activation(q_part[:, 0, 0:TOK], bank[3][:, 0:TOK], ACT.Identity, bias=cols[:, C_BQ:C_BQ + 1]).then_inc(qhi_ready, 1)
            act.wait_ge(wv_done, 1)
            act.activation(wT[:, 2, :], bank[6][:, 0:P], ACT.Copy).then_inc(wvT_ready, 1)

            def head(n, a):
                what, pair = picks[n]
                at = slice(0, N) if what == 0 else slice((what - 1) * TOK, what * TOK)
                act.wait_ge(picked, n + 1)
                act.activation((QA if what else KA)[0:MAXROW, 2 * pair + a, at],
                               bank[PICK_BANK[n]][64 * a:64 * (a + 1), at], ACT.Copy).then_inc(heads_ready, 1)

            def masks(half):
                act.wait_ge(mT_done, half + 1)
                act.activation(maskT[:, :, half * TOK:(half + 1) * TOK], bank[(2, MISC)[half]][:].bitcast(BF16).rearrange("p (i t) -> p i t", i=NI),
                               ACT.Copy).then_inc(maskT_ready, 1)

            def maxima(m):
                rows_m = PARTS * (maxima_of[m][2] - maxima_of[m][1])
                act.wait_ge(nmaxT_done, m + 1)
                act.activation(nmaxT[0:rows_m, m, :], bank[MAXIMA_BANK[m]][0:rows_m, 0:TOK], ACT.Copy).then_inc(nmaxT_ready, 1)

            for pair in range(H // 2):
                for a in range(2):
                    head(2 * pair, a)
                    head(2 * pair + 1, a)
                if pair == 2:
                    maxima(0)
            act.wait_ge(xT_done, 2)
            act.activation(xn1T[:, TOK:T], bank[MISC][:, 0:TOK], ACT.Copy).then_inc(xn1T_ready, 1)
            masks(0)
            maxima(1)

            def exponential(n):
                act.wait_ge(st_done, n + 1)
                if n >= NP_RING:
                    act.wait_ge(pv_done, n // G - 1)
                act.activation(PT[:, n % NP_RING, :], bank[X_BANK[n % len(X_BANK)]][:], ACT.Exp).then_inc(exp_done, 1)

            def output(u):
                act.wait_ge(pv_done, NIP * (u + 1))
                act.activation(O_sb[:, u, :], bank[O_BANK[u % 2]][:, 0:TOK], ACT.Copy).then_inc(o_ready, 1)

            def w1_rounded(e):
                act.wait_ge(in_w1[e], 16)
                act.activation(w1_part[:, e, 0, :], w1_sb[:, e, :], ACT.Copy).then_inc(w1hi_ready, 1)

            def from_misc(done, dst, ready, half, rows_=P):
                act.wait_ge(done, half + 1)
                act.activation(dst, bank[MISC][0:rows_, 0:TOK], ACT.Copy).then_inc(ready, 1)

            for n in range(NU * NX_U):
                if n in pick_at:
                    head(pick_at[n], 0)
                    head(pick_at[n], 1)
                exponential(n)
                if n == 0:
                    act.wait_ge(q_done, 2)
                    act.activation(q_part[:, 0, TOK:T], bank[6][:, TOK:T], ACT.Identity, bias=cols[:, C_BQ:C_BQ + 1]).then_inc(qhi_ready, 1)
                if n == 1:
                    act.wait_ge(v_done, 2)
                    act.wait_ge(va_const_ready, 1)
                    act.activation(Va[:, :, :, 0:DH], bank[5][:].rearrange("p (i h d) -> p i h d", i=NI, d=DH), ACT.Copy).then_inc(va_ready, 1)
                if n == 5:
                    masks(1)
                if n == 7:
                    act.wait_ge(rows_done, 1)
                    act.activation(cols[:, NEARLY:NEARLY + NROWS], bank[MISC][:, 0:NROWS], ACT.Copy).then_inc(cols_ready, 1)
                    act.activation(wT[:, 3, :], bank[MISC][:, P:2 * P], ACT.Copy).then_inc(woT_ready, 1)
                if n % NX_U == 3 and n // NX_U + 1 < NU:
                    maxima(n // NX_U + 2)
                if n % NX_U == 1 and n > NX_U:
                    output(n // NX_U - 1)
                if n % G == 2 and n < G * NE // 2:
                    w1_rounded(n // G)
                if n == 21:
                    from_misc(onatT_done, o_natT[:, 0, :], onatT_ready, 0)
                if n == 26:
                    from_misc(xn2T_done, xn2T[:, 0, :], xn2T_ready, 0)
            for n in range(NHALF * HALF_E):
                if n == 0:
                    act.wait_ge(cols_ready, 1)
                act.wait_ge(f1_done, n + 1)
                if n >= NH_RING:
                    act.wait_ge(f2_done, n - NH_RING + 1)
                act.activation(hid[:, n % NH_RING, :], bank[X_BANK[(NU * NX_U + n) % len(X_BANK)]][:, 0:TOK], ACT.Gelu,
                               bias=cols[:, C_B1 + n % HALF_E:C_B1 + n % HALF_E + 1]).then_inc(hid_ready, 1)
                if n == 1:
                    output(NU - 1)
                if n % FC == 2 and n < FC * NE // 2:
                    w1_rounded(NE // 2 + n // FC)
                if n == 7:
                    from_misc(wexpT_done, wexpT[:, 0, :], wexpT_ready, 0, NE)
                if n == 12:
                    from_misc(onatT_done, o_natT[:, 1, :], onatT_ready, 1)
                if n == 20:
                    from_misc(xn2T_done, xn2T[:, 1, :], xn2T_ready, 1)
                if n == 27:
                    from_misc(wexpT_done, wexpT[:, 1, :], wexpT_ready, 1, NE)

        @block.vector
        def _(dve):
            steps = [0]

            def step(ins):
                steps[0] += 1
                ins.then_inc(dve_step, 1)
                dve.wait_ge(dve_step, steps[0])

            def first_norm(half):
                ts = range(half * HT, (half + 1) * HT)
                dve.wait_ge(in_x[half], 16)
                for t in ts:
                    last = dve.bn_stats(stats[:, t, :], x_sb[:, t, :])
                step(last)
                for t in ts:
                    last = dve.bn_aggr(mv[:, t, :], stats[:, t, :])
                step(last)
                dve.tensor_scalar(var_eps[:, half * HT:(half + 1) * HT], mv[:, half * HT:(half + 1) * HT, 1], EPS, None,
                                  ALU.add).then_inc(var1_ready, 1)

            def first_norm_b(half):
                dve.wait_ge(rstd1_ready, half + 1)
                for t in range(half * HT, (half + 1) * HT):
                    last = dve.tensor_scalar(xn1[:, t, :], x_sb[:, t, :], mv[:, t, 0:1], rstd[:, t:t + 1], ALU.subtract, ALU.mult)
                last.then_inc(xn1_ready, 1)

            def query_rests(half):
                at = slice(half * TOK, (half + 1) * TOK)
                dve.scalar_tensor_tensor(out=q_part[:, 1, at], in0=bank[(3, 6)[half]][:, at], scalar=cols[:, C_BQ:C_BQ + 1],
                                         in1=q_part[:, 0, at].bitcast(F32), op0=ALU.add, op1=ALU.subtract).then_inc(qpart_ready, 1)

            dve.memset(warm[:], 0.0).then_inc(warm_ready, 1)
            dve.memset(ones_row[:], 1.0)
            dve.memset(pick_q[:].bitcast(F32), 0.0).then_inc(pick_zero, 1)
            dve.memset(pick_k[:].bitcast(F32), 0.0).then_inc(pick_zero, 1)
            first_norm(0)
            dve.wait_ge(pick_zero, 2)
            dve.wait_ge(ident_ready, 1)
            head_rows = ident[:].rearrange("p (h d) -> p h d", d=DH).unsqueeze(2).broadcast_to([P, H, 2, DH])
            for part in range(PARTS):
                q_cols = pick_q[:, part, :, :].rearrange("p h (c r d) -> p h c r d", c=2, d=DH)[:, :, part, :, :]
                k_cols = pick_k[:, part, :, :].rearrange("p h (r c d) -> p h r c d", c=2, d=DH)[:, :, :, part, :]
                dve.tensor_copy(q_cols, head_rows).then_inc(pick_ready, 1)
                dve.tensor_copy(k_cols, head_rows).then_inc(pick_ready, 1)
            first_norm_b(0)
            dve.wait_ge(wk_done, 1)
            dve.tensor_copy(wT[:, 1, :], bank[1][:, P:2 * P]).then_inc(wkT_ready, 1)
            dve.wait_ge(wq_done, 1)
            dve.tensor_scalar(wT[:, 0, :], bank[6][:, 0:P], float(DH) ** -0.5, None, ALU.mult).then_inc(wqT_ready, 1)
            dve.wait_ge(xT_done, 1)
            dve.tensor_copy(xn1T[:, 0:TOK], bank[0][:, 0:TOK]).then_inc(xn1T_ready, 1)
            first_norm(1)
            dve.wait_ge(cols_early_ready, 2)
            dve.wait_ge(khi_ready, 1)
            dve.scalar_tensor_tensor(out=k_part[:, 1, :], in0=bank[4][:], scalar=cols[:, C_BK:C_BK + 1],
                                     in1=k_part[:, 0, :].bitcast(F32), op0=ALU.add, op1=ALU.subtract).then_inc(kpart_ready, 1)
            dve.wait_ge(qhi_ready, 1)
            query_rests(0)
            dve.wait_ge(in_adj, 16)
            for t in range(HT):
                dve.tensor_scalar(maskb[:, t, :], adj_sb[:, t, :], 0.0, MASKED, ALU.is_equal, ALU.mult).then_inc(maskb_ready, 1)
            first_norm_b(1)

            def maximum(n):
                u, r = n // NS_U, n % NS_U
                t, j = tile_of(r)
                if n == 0:
                    dve.wait_ge(maskb_ready, HT)
                if n == NG * NS_U:
                    dve.wait_ge(maskb_late_ready, HT)
                dve.wait_ge(s_done, n + 1)
                dve.tensor_tensor_reduce(out=junk[:, n % 2, :], in0=bank[S_BANK[n % 2]][:],
                                         in1=maskb[:, unit[u][0] * HT + t, :], scale=1.0, scalar=-3e38,
                                         op0=ALU.add, op1=ALU.max, accum_out=mx[:, u, t * G + j:t * G + j + 1]).then_inc(s_used, 1)

            def negative_maxima(m):
                u, a, b = maxima_of[m]
                dve.wait_ge(s_used, NS_U * u + HT * b)
                nm = nmax[:, u, :].rearrange("p (t j) -> p t j", j=G)[:, :, a:b]
                parts = [nmax_part[:, m, :, part * (b - a):(part + 1) * (b - a)] for part in range(PARTS)]
                step(dve.tensor_scalar(nm, mx[:, u, :].rearrange("p (t j) -> p t j", j=G)[:, :, a:b], LOWEST_MAX, -1.0, ALU.max, ALU.mult))
                step(dve.tensor_copy(parts[0], nm))
                dve.tensor_tensor(parts[1], nm, parts[0].bitcast(F32), ALU.subtract).then_inc(nmax_ready, 1)

            def normalise(u):
                half, g = unit[u]
                dve.wait_ge(oT_done, u + 1)
                o = bank[MISC][:, 0:TOK].rearrange("p (t j r) -> p t j r", t=HT, j=G)
                d = den[:, u, :].rearrange("p (t j) -> p t j", j=G)
                step(dve.tensor_scalar(d, o[:, :, :, DH], TINY, None, ALU.max))
                step(dve.reciprocal(rden[:, u, :], den[:, u, :]))
                for t in range(HT):
                    r = rden[:, u, t * G:(t + 1) * G].unsqueeze(2).broadcast_to([P, G, DH])
                    last = dve.tensor_tensor(o_nat[:, half, t, G * g:G * g + G, :], o[:, t, :, 0:DH], r, ALU.mult)
                last.then_inc(onat_ready, 1)

            def second_norms(half):
                ts = slice(half * HT, (half + 1) * HT)
                dve.wait_ge(proj_done, half + 1)
                dve.wait_ge(xb_ready, 1)
                dve.tensor_tensor(x2[:, ts, :], bank[MISC][:, 0:TOK].rearrange("p (t d) -> p t d", d=D), xb[:, ts, :],
                                  ALU.add).then_inc(x2_ready, 1)
                dve.wait_ge(x2_ready, half + 1)
                for t in range(half * HT, (half + 1) * HT):
                    last = dve.bn_stats(stats2[:, t, :], x2[:, t, :])
                step(last)
                for t in range(half * HT, (half + 1) * HT):
                    last = dve.bn_aggr(mv2[:, t, :], stats2[:, t, :])
                step(last)
                dve.tensor_scalar(vw[:, ts, 0], mv2[:, ts, 1], EPS, None, ALU.add)
                dve.tensor_scalar(vw[:, ts, 1], mv2[:, ts, 1], 1.0 + EPS, EPS * EPS, ALU.mult, ALU.add).then_inc(vw_ready, 1)

            def second_norms_b(half):
                ts = slice(half * HT, (half + 1) * HT)
                dve.wait_ge(rvw_ready, 2 * half + 1)
                for t in range(half * HT, (half + 1) * HT):
                    last = dve.tensor_scalar(xn2[:, t, :], x2[:, t, :], mv2[:, t, 0:1], rvw[:, t, 1:2], ALU.subtract, ALU.mult)
                last.then_inc(xn2_ready, 1)
                step(dve.tensor_tensor(sw[:, ts], vw[:, ts, 1], rvw[:, ts, 1], ALU.mult))
                dve.wait_ge(rvw_ready, 2 * half + 2)
                step(dve.tensor_tensor(sdb[:, ts], sw[:, ts], rvw[:, ts, 0], ALU.mult))

            def router(half):
                ts, tiles = slice(half * HT, (half + 1) * HT), range(half * HT, (half + 1) * HT)
                dve.wait_ge(in_bias_bc, 32)
                dve.wait_ge(logits_done, half + 1)
                for t in tiles:
                    k = t - half * HT
                    last = dve.scalar_tensor_tensor(out=logits[:, t, :], in0=bank[MISC][:, k * NE:(k + 1) * NE],
                                                    scalar=sdb[:, t:t + 1], in1=br_bc[:], op0=ALU.mult, op1=ALU.add)
                last.then_inc(logits_used, 1)
                dve.wait_ge(logits_used, half + 1)
                for t in tiles:
                    last = dve.max(top[:, t, :], logits[:, t, :])
                step(last)
                dve.tensor_tensor(gap[:, ts], top[:, ts, 1], top[:, ts, 0], ALU.subtract).then_inc(gap_ready, 1)
                for t in tiles:
                    last = dve.max_index(top_at[:, t, :], top[:, t, :], logits[:, t, :])
                step(last)
                dve.tensor_copy(top_no[:, ts, :], top_at[:, ts, 0:2])

            def router_b(half):
                ts, tiles = slice(half * HT, (half + 1) * HT), range(half * HT, (half + 1) * HT)
                dve.wait_ge(egap_ready, half + 1)
                step(dve.tensor_scalar(dgap[:, ts], egap[:, ts], 1.0, None, ALU.add))
                step(dve.reciprocal(wtop[:, ts, 0], dgap[:, ts]))
                step(dve.tensor_tensor(wtop[:, ts, 1], wtop[:, ts, 0], egap[:, ts], ALU.mult))
                dve.wait_ge(expert_no_ready, 1)
                for t in tiles:
                    dve.tensor_scalar(wfirst[:, t, :], expert_no[:], top_no[:, t, 0:1], wtop[:, t, 0:1], ALU.is_equal, ALU.mult)
                    last = dve.tensor_scalar(wsecond[:, t, :], expert_no[:], top_no[:, t, 1:2], wtop[:, t, 1:2], ALU.is_equal, ALU.mult)
                step(last)
                dve.tensor_tensor(wexp[:, ts, :], wfirst[:, ts, :], wsecond[:, ts, :], ALU.add).then_inc(wexp_ready, 1)

            def start_sum(half):
                ts = slice(half * HT, (half + 1) * HT)
                dve.wait_ge(b2_done, half + 1)
                dve.tensor_tensor(acc[:, 1, ts, :], bank[MISC][:, 0:TOK].rearrange("p (t d) -> p t d", d=D), x2[:, ts, :],
                                  ALU.add).then_inc(acc0_ready, 1)
                dve.wait_ge(acc0_ready, half + 1)

            def expert_in(m):
                half, e = m // NE, m % NE
                if e == 0:
                    dve.wait_ge(cols_ready, 1)
                    dve.wait_ge(xn2T_ready, half + 1)
                if m >= NXE_RING:
                    dve.wait_ge(f1_done, FC * (m - NXE_RING + 1))
                z = m % NXE_RING
                step(dve.tensor_scalar(xe[:, z, :], xn2T[:, half, :], cols[:, C_G + e:C_G + e + 1], cols[:, C_B + e:C_B + e + 1],
                                       ALU.mult, ALU.add))
                step(dve.tensor_copy(xe_part[:, z, 0, :], xe[:, z, :]))
                dve.tensor_tensor(xe_part[:, z, 1, :], xe[:, z, :], xe_part[:, z, 0, :].bitcast(F32), ALU.subtract).then_inc(xe_ready, 1)

            def product(m, k):
                return bank[LAST_BANK[k]][:, 0:P] if m == LAST else bank[S_BANK[m % 2]][:, k * P:(k + 1) * P]

            def add_expert(m):
                half, e = m // NE, m % NE
                if e == 0:
                    dve.wait_ge(wexp_ready, half + 1)
                if m < LAST:
                    dve.wait_ge(f2_done, FC * (m + 1))
                for k in range(HT):
                    t = half * HT + k
                    if m == LAST:
                        dve.wait_ge(last_done, k + 1)
                    last = dve.scalar_tensor_tensor(out=acc[:, e % 2, t, :], in0=product(m, k),
                                                    scalar=wexp[:, t, e:e + 1], in1=acc[:, 1 - e % 2, t, :],
                                                    op0=ALU.mult, op1=ALU.add)
                    if m == LAST and k < HT - 1:
                        last.then_inc(last_added, 1)
                last.then_inc(y_used, 1)
                dve.wait_ge(y_used, m + 1)

            for n in range(NU * NS_U):
                maximum(n)
                if n == NS_U // 2 - 1:
                    negative_maxima(0)
                if n % NS_U == NS_U - 1:
                    negative_maxima(n // NS_U + 1)
                if n == NS_U + 3:
                    dve.wait_ge(qhi_ready, 2)
                    query_rests(1)
                if n == LEAD + 13:
                    normalise(0)
            normalise(1)
            second_norms(0)
            second_norms_b(0)
            expert_in(0)
            expert_in(1)
            router(0)
            expert_in(2)
            router_b(0)
            normalise(2)
            normalise(3)
            expert_in(NXE_RING)
            start_sum(0)
            for m in range(NHALF * NE):
                if 0 < m < NHALF * NE - NXE_RING:
                    expert_in(m + NXE_RING)
                if m == 4:
                    router_b(1)
                add_expert(m)
                if m == 1:
                    second_norms(1)
                if m == 2:
                    second_norms_b(1)
                if m == 3:
                    router(1)
                if m == 6:
                    start_sum(1)


_INS = ['x', 'adj', 'L0_gnn_h_neigh', 'L0_gnn_Wq', 'L0_gnn_bq', 'L0_gnn_Wk', 'L0_gnn_bk', 'L0_gnn_Wv', 'L0_gnn_bv',
        'L0_gnn_Wo', 'L0_gnn_bo', 'L0_gnn_E', 'L0_ffn_Wr', 'L0_ffn_br', 'L0_ffn_ln_g', 'L0_ffn_ln_b', 'L0_ffn_W1',
        'L0_ffn_b1', 'L0_ffn_W2', 'L0_ffn_b2']
_OUTS = [((512, 128), 'float32')]


def kernel(**inputs):
    import numpy as _np
    import concourse.bacc as _bacc
    from concourse import mybir as _mybir
    from concourse.bass_utils import run_bass_kernel_spmd as _run

    nc = _bacc.Bacc("TRN2", target_bir_lowering=False, num_devices=1)
    arrays, args = {}, []
    for name in _INS:
        a = _np.ascontiguousarray(inputs[name])
        arrays[f"in_{name}_dram"] = a
        args.append(nc.dram_tensor(f"in_{name}_dram", a.shape, _mybir.dt.from_np(a.dtype), kind="ExternalInput").ap())
    for i, (shape, dtype) in enumerate(_OUTS):
        dt = _mybir.dt.from_np(_np.dtype(dtype))
        args.append(nc.dram_tensor(f"out_{i}_dram", shape, dt, kind="ExternalOutput").ap())
    gnn_ffn_kernel(nc, *args)
    r = _run(nc, [arrays], core_ids=[0])
    got = tuple(r.results[0][f"out_{i}_dram"] for i in range(len(_OUTS)))
    return got[0]
```
